# Optimizing a Trainium2 kernel written in Bass

```python
import numpy as np
import jax
import jax.numpy as jnp

def _softmax(x, axis=-1):
    return jax.nn.softmax(x, axis=axis)

def _gelu(x):
    return jax.nn.gelu(x, approximate=True)

def _silu(x):
    return jax.nn.silu(x)

def _sigmoid(x):
    return jax.nn.sigmoid(x)

def _layernorm(x, axis=-1, eps=1e-05):
    m = jnp.mean(x, axis=axis, keepdims=True)
    v = jnp.var(x, axis=axis, keepdims=True)
    return (x - m) / jnp.sqrt(v + eps)

def _scatter_add(tgt, idx, src, axis=0):
    return tgt.at[idx].add(src)

def _segment_sum(src, seg, n):
    return jax.ops.segment_sum(src, seg, n)
kernel_name = 'mk_dlrm_tower_d1_rec_r8_fc60b7'

def setup_inputs(seed: int=0):
    np.random.seed(seed)
    _w = jnp.asarray

    def _rec_inputs():
        import jax
        import jax.numpy as jnp
        _tk = jax.random.key(seed)
        dense_ctx = jax.random.normal(jax.random.fold_in(_tk, 190), (512, 16), jnp.float32)
        ids = jnp.stack([jax.random.randint(jax.random.fold_in(_tk, 200 + f), (512,), 0, v, jnp.int32) for f, v in enumerate([1250, 1000, 1250, 125000, 1250, 1000, 12500, 1000, 12500, 1000, 1250, 1250, 1000, 1000, 125000, 1250, 1250, 1000, 1250, 1250, 1000, 1250, 12500, 125000, 125000, 1250, 1000, 1000, 125000, 125000, 1000, 12500, 125000, 12500, 1250, 1000, 12500, 125000, 12500])], axis=1)
        tbl_0 = 0.05 * jax.random.normal(jax.random.fold_in(_tk, 500 + 0), (1250, 16), jnp.float32)
        tbl_1 = 0.05 * jax.random.normal(jax.random.fold_in(_tk, 500 + 1), (1000, 16), jnp.float32)
        tbl_2 = 0.05 * jax.random.normal(jax.random.fold_in(_tk, 500 + 2), (1250, 16), jnp.float32)
        tbl_3 = 0.05 * jax.random.normal(jax.random.fold_in(_tk, 500 + 3), (125000, 16), jnp.float32)
        tbl_4 = 0.05 * jax.random.normal(jax.random.fold_in(_tk, 500 + 4), (1250, 16), jnp.float32)
        tbl_5 = 0.05 * jax.random.normal(jax.random.fold_in(_tk, 500 + 5), (1000, 16), jnp.float32)
        tbl_6 = 0.05 * jax.random.normal(jax.random.fold_in(_tk, 500 + 6), (12500, 16), jnp.float32)
        tbl_7 = 0.05 * jax.random.normal(jax.random.fold_in(_tk, 500 + 7), (1000, 16), jnp.float32)
        tbl_8 = 0.05 * jax.random.normal(jax.random.fold_in(_tk, 500 + 8), (12500, 16), jnp.float32)
        tbl_9 = 0.05 * jax.random.normal(jax.random.fold_in(_tk, 500 + 9), (1000, 16), jnp.float32)
        tbl_10 = 0.05 * jax.random.normal(jax.random.fold_in(_tk, 500 + 10), (1250, 16), jnp.float32)
        tbl_11 = 0.05 * jax.random.normal(jax.random.fold_in(_tk, 500 + 11), (1250, 16), jnp.float32)
        tbl_12 = 0.05 * jax.random.normal(jax.random.fold_in(_tk, 500 + 12), (1000, 16), jnp.float32)
        tbl_13 = 0.05 * jax.random.normal(jax.random.fold_in(_tk, 500 + 13), (1000, 16), jnp.float32)
        tbl_14 = 0.05 * jax.random.normal(jax.random.fold_in(_tk, 500 + 14), (125000, 16), jnp.float32)
        tbl_15 = 0.05 * jax.random.normal(jax.random.fold_in(_tk, 500 + 15), (1250, 16), jnp.float32)
        tbl_16 = 0.05 * jax.random.normal(jax.random.fold_in(_tk, 500 + 16), (1250, 16), jnp.float32)
        tbl_17 = 0.05 * jax.random.normal(jax.random.fold_in(_tk, 500 + 17), (1000, 16), jnp.float32)
        tbl_18 = 0.05 * jax.random.normal(jax.random.fold_in(_tk, 500 + 18), (1250, 16), jnp.float32)
        tbl_19 = 0.05 * jax.random.normal(jax.random.fold_in(_tk, 500 + 19), (1250, 16), jnp.float32)
        tbl_20 = 0.05 * jax.random.normal(jax.random.fold_in(_tk, 500 + 20), (1000, 16), jnp.float32)
        tbl_21 = 0.05 * jax.random.normal(jax.random.fold_in(_tk, 500 + 21), (1250, 16), jnp.float32)
        tbl_22 = 0.05 * jax.random.normal(jax.random.fold_in(_tk, 500 + 22), (12500, 16), jnp.float32)
        tbl_23 = 0.05 * jax.random.normal(jax.random.fold_in(_tk, 500 + 23), (125000, 16), jnp.float32)
        tbl_24 = 0.05 * jax.random.normal(jax.random.fold_in(_tk, 500 + 24), (125000, 16), jnp.float32)
        tbl_25 = 0.05 * jax.random.normal(jax.random.fold_in(_tk, 500 + 25), (1250, 16), jnp.float32)
        tbl_26 = 0.05 * jax.random.normal(jax.random.fold_in(_tk, 500 + 26), (1000, 16), jnp.float32)
        tbl_27 = 0.05 * jax.random.normal(jax.random.fold_in(_tk, 500 + 27), (1000, 16), jnp.float32)
        tbl_28 = 0.05 * jax.random.normal(jax.random.fold_in(_tk, 500 + 28), (125000, 16), jnp.float32)
        tbl_29 = 0.05 * jax.random.normal(jax.random.fold_in(_tk, 500 + 29), (125000, 16), jnp.float32)
        tbl_30 = 0.05 * jax.random.normal(jax.random.fold_in(_tk, 500 + 30), (1000, 16), jnp.float32)
        tbl_31 = 0.05 * jax.random.normal(jax.random.fold_in(_tk, 500 + 31), (12500, 16), jnp.float32)
        tbl_32 = 0.05 * jax.random.normal(jax.random.fold_in(_tk, 500 + 32), (125000, 16), jnp.float32)
        tbl_33 = 0.05 * jax.random.normal(jax.random.fold_in(_tk, 500 + 33), (12500, 16), jnp.float32)
        tbl_34 = 0.05 * jax.random.normal(jax.random.fold_in(_tk, 500 + 34), (1250, 16), jnp.float32)
        tbl_35 = 0.05 * jax.random.normal(jax.random.fold_in(_tk, 500 + 35), (1000, 16), jnp.float32)
        tbl_36 = 0.05 * jax.random.normal(jax.random.fold_in(_tk, 500 + 36), (12500, 16), jnp.float32)
        tbl_37 = 0.05 * jax.random.normal(jax.random.fold_in(_tk, 500 + 37), (125000, 16), jnp.float32)
        tbl_38 = 0.05 * jax.random.normal(jax.random.fold_in(_tk, 500 + 38), (12500, 16), jnp.float32)
        _rk = jax.random.fold_in(_tk, 7)
        W_top1 = 0.0606339 * jax.random.normal(jax.random.fold_in(_tk, 801), (272, 512), jnp.float32)
        W_top2 = 0.0441942 * jax.random.normal(jax.random.fold_in(_tk, 802), (512, 256), jnp.float32)
        W_top3 = 0.0625 * jax.random.normal(jax.random.fold_in(_tk, 803), (256, 1), jnp.float32)
        b_top1 = jnp.zeros((512,), jnp.float32)
        b_top2 = jnp.zeros((256,), jnp.float32)
        return (dense_ctx, ids, tbl_0, tbl_1, tbl_2, tbl_3, tbl_4, tbl_5, tbl_6, tbl_7, tbl_8, tbl_9, tbl_10, tbl_11, tbl_12, tbl_13, tbl_14, tbl_15, tbl_16, tbl_17, tbl_18, tbl_19, tbl_20, tbl_21, tbl_22, tbl_23, tbl_24, tbl_25, tbl_26, tbl_27, tbl_28, tbl_29, tbl_30, tbl_31, tbl_32, tbl_33, tbl_34, tbl_35, tbl_36, tbl_37, tbl_38, W_top1, b_top1, W_top2, b_top2, W_top3)
    dense_ctx, ids, tbl_0, tbl_1, tbl_2, tbl_3, tbl_4, tbl_5, tbl_6, tbl_7, tbl_8, tbl_9, tbl_10, tbl_11, tbl_12, tbl_13, tbl_14, tbl_15, tbl_16, tbl_17, tbl_18, tbl_19, tbl_20, tbl_21, tbl_22, tbl_23, tbl_24, tbl_25, tbl_26, tbl_27, tbl_28, tbl_29, tbl_30, tbl_31, tbl_32, tbl_33, tbl_34, tbl_35, tbl_36, tbl_37, tbl_38, W_top1, b_top1, W_top2, b_top2, W_top3 = _rec_inputs()

    def _L0_rec_setup():
        import jax, jax.numpy as jnp
        import numpy as np
        B, F, D = (1024, 39, 16)
        HIDDEN = [128, 128, 128]

        def _cin(x, Ws, bs):
            F0 = x.shape[1]
            h = x
            outs = []
            n = len(Ws)
            for i, (W, b) in enumerate(zip(Ws, bs)):
                L = W.shape[-1]
                Fk = h.shape[1]
                Wr = W.reshape(F0, Fk, L)
                z = jnp.einsum('bfd,bgd->bfgd', x, h)
                cur = jax.nn.relu(jnp.einsum('bfgd,fgl->bld', z, Wr) + b[None, :, None])
                if i != n - 1:
                    h = cur[:, :L // 2]
                    direct = cur[:, L // 2:]
                else:
                    direct = cur
                outs.append(direct)
            return jnp.concatenate(outs, axis=1).sum(-1)
        key = jax.random.key(seed)
        ks = jax.random.split(key, 8)
        x = jax.random.normal(ks[0], (B, F, D), dtype=jnp.float32)
        field_nums = [F]
        Ws, bs = ([], [])
        for i, L in enumerate(HIDDEN):
            fan_in = field_nums[0] * field_nums[-1]
            lim = np.sqrt(6.0 / fan_in)
            Ws.append(jax.random.uniform(ks[1 + i], (fan_in, L), jnp.float32, -lim, lim))
            bs.append(jnp.zeros((L,), jnp.float32))
            field_nums.append(L // 2)
        return {'x': x, 'W0': Ws[0], 'W1': Ws[1], 'W2': Ws[2], 'b0': bs[0], 'b1': bs[1], 'b2': bs[2]}
    _L0_rec_all = _L0_rec_setup()
    _L0_rec_in = {k: v for k, v in _L0_rec_all.items() if k in ('W0', 'W1', 'W2', 'b0', 'b1', 'b2')}
    del _L0_rec_all
    return {'dense_ctx': dense_ctx, 'ids': ids, 'tbl_0': tbl_0, 'tbl_1': tbl_1, 'tbl_2': tbl_2, 'tbl_3': tbl_3, 'tbl_4': tbl_4, 'tbl_5': tbl_5, 'tbl_6': tbl_6, 'tbl_7': tbl_7, 'tbl_8': tbl_8, 'tbl_9': tbl_9, 'tbl_10': tbl_10, 'tbl_11': tbl_11, 'tbl_12': tbl_12, 'tbl_13': tbl_13, 'tbl_14': tbl_14, 'tbl_15': tbl_15, 'tbl_16': tbl_16, 'tbl_17': tbl_17, 'tbl_18': tbl_18, 'tbl_19': tbl_19, 'tbl_20': tbl_20, 'tbl_21': tbl_21, 'tbl_22': tbl_22, 'tbl_23': tbl_23, 'tbl_24': tbl_24, 'tbl_25': tbl_25, 'tbl_26': tbl_26, 'tbl_27': tbl_27, 'tbl_28': tbl_28, 'tbl_29': tbl_29, 'tbl_30': tbl_30, 'tbl_31': tbl_31, 'tbl_32': tbl_32, 'tbl_33': tbl_33, 'tbl_34': tbl_34, 'tbl_35': tbl_35, 'tbl_36': tbl_36, 'tbl_37': tbl_37, 'tbl_38': tbl_38, 'W_top1': W_top1, 'b_top1': b_top1, 'W_top2': W_top2, 'b_top2': b_top2, 'W_top3': W_top3, 'L0_rec_W0': _L0_rec_in['W0'], 'L0_rec_W1': _L0_rec_in['W1'], 'L0_rec_W2': _L0_rec_in['W2'], 'L0_rec_b0': _L0_rec_in['b0'], 'L0_rec_b1': _L0_rec_in['b1'], 'L0_rec_b2': _L0_rec_in['b2']}

def reference(dense_ctx, ids, tbl_0, tbl_1, tbl_2, tbl_3, tbl_4, tbl_5, tbl_6, tbl_7, tbl_8, tbl_9, tbl_10, tbl_11, tbl_12, tbl_13, tbl_14, tbl_15, tbl_16, tbl_17, tbl_18, tbl_19, tbl_20, tbl_21, tbl_22, tbl_23, tbl_24, tbl_25, tbl_26, tbl_27, tbl_28, tbl_29, tbl_30, tbl_31, tbl_32, tbl_33, tbl_34, tbl_35, tbl_36, tbl_37, tbl_38, W_top1, b_top1, W_top2, b_top2, W_top3, L0_rec_W0, L0_rec_W1, L0_rec_W2, L0_rec_b0, L0_rec_b1, L0_rec_b2):
    import jax
    import jax.numpy as jnp

    def _L0_rec_ref(x, W0, W1, W2, b0, b1, b2):
        import jax, jax.numpy as jnp
        import numpy as np
        B, F, D = (1024, 39, 16)
        HIDDEN = [128, 128, 128]

        def _cin(x, Ws, bs):
            F0 = x.shape[1]
            h = x
            outs = []
            n = len(Ws)
            for i, (W, b) in enumerate(zip(Ws, bs)):
                L = W.shape[-1]
                Fk = h.shape[1]
                Wr = W.reshape(F0, Fk, L)
                z = jnp.einsum('bfd,bgd->bfgd', x, h)
                cur = jax.nn.relu(jnp.einsum('bfgd,fgl->bld', z, Wr) + b[None, :, None])
                if i != n - 1:
                    h = cur[:, :L // 2]
                    direct = cur[:, L // 2:]
                else:
                    direct = cur
                outs.append(direct)
            return jnp.concatenate(outs, axis=1).sum(-1)
        return _cin(x, [W0, W1, W2], [b0, b1, b2])
    e = jnp.stack([tbl_0[ids[:, 0]], tbl_1[ids[:, 1]], tbl_2[ids[:, 2]], tbl_3[ids[:, 3]], tbl_4[ids[:, 4]], tbl_5[ids[:, 5]], tbl_6[ids[:, 6]], tbl_7[ids[:, 7]], tbl_8[ids[:, 8]], tbl_9[ids[:, 9]], tbl_10[ids[:, 10]], tbl_11[ids[:, 11]], tbl_12[ids[:, 12]], tbl_13[ids[:, 13]], tbl_14[ids[:, 14]], tbl_15[ids[:, 15]], tbl_16[ids[:, 16]], tbl_17[ids[:, 17]], tbl_18[ids[:, 18]], tbl_19[ids[:, 19]], tbl_20[ids[:, 20]], tbl_21[ids[:, 21]], tbl_22[ids[:, 22]], tbl_23[ids[:, 23]], tbl_24[ids[:, 24]], tbl_25[ids[:, 25]], tbl_26[ids[:, 26]], tbl_27[ids[:, 27]], tbl_28[ids[:, 28]], tbl_29[ids[:, 29]], tbl_30[ids[:, 30]], tbl_31[ids[:, 31]], tbl_32[ids[:, 32]], tbl_33[ids[:, 33]], tbl_34[ids[:, 34]], tbl_35[ids[:, 35]], tbl_36[ids[:, 36]], tbl_37[ids[:, 37]], tbl_38[ids[:, 38]]], axis=1)
    z = _L0_rec_ref(e, L0_rec_W0, L0_rec_W1, L0_rec_W2, L0_rec_b0, L0_rec_b1, L0_rec_b2)
    z = z.reshape(z.shape[0], -1)
    h = jnp.concatenate([z, dense_ctx], axis=1)
    h = jnp.maximum(h @ W_top1 + b_top1, 0.0)
    h = jnp.maximum(h @ W_top2 + b_top2, 0.0)
    y = h @ W_top3
    return y

_drawn_inputs = setup_inputs


def setup_inputs(seed=0):
    import zlib

    import numpy as np

    out = dict(_drawn_inputs(seed))
    spreads = {'b_top1': (0.0, 2.0),
     'b_top2': (0.0, 2.0),
     'L0_rec_b0': (0.0, 0.331),
     'L0_rec_b1': (0.0, 0.487),
     'L0_rec_b2': (0.0, 0.8)}
    factors = {'tbl_0': 8.0,
     'tbl_1': 8.0,
     'tbl_2': 8.0,
     'tbl_3': 8.0,
     'tbl_4': 8.0,
     'tbl_5': 8.0,
     'tbl_6': 8.0,
     'tbl_7': 8.0,
     'tbl_8': 8.0,
     'tbl_9': 8.0,
     'tbl_10': 8.0,
     'tbl_11': 8.0,
     'tbl_12': 8.0,
     'tbl_13': 8.0,
     'tbl_14': 8.0,
     'tbl_15': 8.0,
     'tbl_16': 8.0,
     'tbl_17': 8.0,
     'tbl_18': 8.0,
     'tbl_19': 8.0,
     'tbl_20': 8.0,
     'tbl_21': 8.0,
     'tbl_22': 8.0,
     'tbl_23': 8.0,
     'tbl_24': 8.0,
     'tbl_25': 8.0,
     'tbl_26': 8.0,
     'tbl_27': 8.0,
     'tbl_28': 8.0,
     'tbl_29': 8.0,
     'tbl_30': 8.0,
     'tbl_31': 8.0,
     'tbl_32': 8.0,
     'tbl_33': 8.0,
     'tbl_34': 8.0,
     'tbl_35': 8.0,
     'tbl_36': 8.0,
     'tbl_37': 8.0,
     'tbl_38': 8.0,
     'L0_rec_W0': 8.0,
     'L0_rec_W1': 5.653,
     'L0_rec_W2': 4.807,
     'dense_ctx': 8.0}
    for name, (base, spread) in spreads.items():
        noise = np.random.default_rng([zlib.crc32(name.encode()), seed]).standard_normal(out[name].shape)
        drawn = base * np.exp(spread * noise) if base else spread * noise
        out[name] = jnp.asarray(drawn.astype(out[name].dtype))
    for name, factor in factors.items():
        out[name] = (out[name] * factor).astype(out[name].dtype)
    return out
```

```python
from contextlib import ExitStack
from itertools import cycle

import concourse.bass as bass
import concourse.mybir as mybir

F32 = mybir.dt.float32
I32 = mybir.dt.int32
ALU = mybir.AluOpType
ACT = mybir.ActivationFunctionType
AX_X = mybir.AxisListType.X

P = 128
F = 39
D = 16
B = 512
CB = 32
CN = CB * D
CHUNKS = B // CB
PAIRS = CHUNKS // 2
HALF = 64
L = 128
OFFS = 20
J0 = 3
R0 = J0 * F
T0 = -(-OFFS // J0)
R0_LAST = (OFFS - J0 * (T0 - 1)) * F
T1 = -(-F // 2)
G = 4
XROWS = 60
NG = 10
GF = P // CB
RING = 4
TOP = 512
TOP2 = 256
DENSE = 16


def group_sizes(tiles):
    return [min(G, tiles - t) for t in range(0, tiles, G)]


G0 = group_sizes(T0)
G1 = group_sizes(T1)
GC = len(G0) + 2 * len(G1)


def build(nc, table, ids, bases, w0a, w0b, w1, w2, biases, denseT, wt1, bt1, wt2, bt2, wt3, out):
    ctx = ExitStack()
    with ctx:
        def sb(name, shape, dt=F32):
            return ctx.enter_context(nc.sbuf_tensor(name, shape, dt))

        def bank(name):
            return ctx.enter_context(nc.psum_tensor(name, [P, CN], F32))

        def sem(name):
            return ctx.enter_context(nc.semaphore(name))

        xT = [nc.dram_tensor(f"xT{q}", [XROWS, CN], F32, kind="Internal") for q in range(2)]

        ids_sb = sb("ids_sb", [P, CHUNKS * NG], I32)
        bases_sb = sb("bases_sb", [P, NG], I32)
        rows_sb = sb("rows_sb", [P, 2, NG], I32)
        emb = sb("emb", [P, 2, NG, D])
        xa = sb("xa", [R0, CN])
        xb = sb("xb", [R0, T0, CN])
        xrep = sb("xrep", [P, 2, T1, CN])
        z = sb("z", [P, RING, G, CN])
        w0_sb = sb("w0_sb", [R0, T0, L])
        w0b_sb = sb("w0b_sb", [R0, T0, L])
        w1_sb = sb("w1_sb", [P, T1, L])
        w2_sb = sb("w2_sb", [P, T1, L])
        bias_sb = sb("bias_sb", [P, 3])
        direct01 = sb("direct01", [P, 2, CN])
        direct2 = sb("direct2", [P, CN])
        sums01 = sb("sums01", [P, B])
        sums2 = sb("sums2", [P, B])
        dense_sb = sb("dense_sb", [DENSE, B])
        wt1_sb = sb("wt1_sb", [P, 2, TOP])
        wt1d_sb = sb("wt1d_sb", [DENSE, TOP])
        wt2_sb = sb("wt2_sb", [P, TOP // P, TOP2])
        wt3_sb = sb("wt3_sb", [P, TOP2 // P])
        bt1_sb = sb("bt1_sb", [P, TOP // P])
        bt2_sb = sb("bt2_sb", [P, TOP2 // P])
        top1 = sb("top1", [P, TOP // P, B])
        top2 = sb("top2", [P, TOP2 // P, B])
        y_sb = sb("y_sb", [1, B])

        acc = [bank("acc0"), bank("acc1")]
        h1 = bank("h1")
        h2 = bank("h2")
        mlp_acc = [bank(f"mlp_acc{i}") for i in range(4)]

        ids_in = sem("ids_in")
        small_in = sem("small_in")
        w0_in = sem("w0_in")
        w1_in = sem("w1_in")
        w2_in = sem("w2_in")
        top_in = sem("top_in")
        w0_summed = sem("w0_summed")
        rows_ready = sem("rows_ready")
        gathers_begun = sem("gathers_begun")
        copies_begun = sem("copies_begun")
        gathered = [sem(f"gathered{q}") for q in range(2)]
        xT_written = [sem(f"xT_written{q}") for q in range(2)]
        x0_loaded = sem("x0_loaded")
        xrep_loaded = [[sem(f"xrep_loaded{q}_{g}") for g in range(len(G1))] for q in range(2)]
        z_made = sem("z_made")
        z_free = sem("z_free")
        h1_ready = sem("h1_ready")
        h2_ready = sem("h2_ready")
        direct01_ready = sem("direct01_ready")
        direct2_ready = sem("direct2_ready")
        sums01_done = sem("sums01_done")
        sums2_done = sem("sums2_done")
        top_done = sem("top_done")
        top_relu = sem("top_relu")
        y_done = sem("y_done")
        y_out = sem("y_out")

        block = ctx.enter_context(nc.Block())

        N0, N1 = len(G0), len(G1)

        def first_group(layer, c, last=False):
            if layer == 0:
                return (c - 1) * GC + N0 + N1 if not (isinstance(c, int) and c == 0) else 0
            if layer == 1:
                return c * GC + N0
            return c * GC + 2 * N0 + N1 - (N0 if last else 0)

        def over_pairs(eng, pair):
            pair(0, True, False)
            with eng.Fori(1, PAIRS - 1) as i:
                pair(i, False, False)
            pair(PAIRS - 1, False, True)

        @block.sync
        def _(sp):
            sp.dma_start(ids_sb[:], ids).then_inc(ids_in, 16)
            sp.dma_start(bases_sb[:], bases).then_inc(ids_in, 16)
            sp.dma_start(bias_sb[:], biases).then_inc(small_in, 16)
            sp.dma_start(w0_sb[:], w0a).then_inc(w0_in, 16)
            sp.dma_start(w0b_sb[:], w0b).then_inc(w0_in, 16)

            def transpose_x(i, q):
                sp.wait_ge(gathered[q], (i + 1) * (NG * 16))
                sp.sem_inc(copies_begun, 1)
                if not isinstance(i, int):
                    sp.wait_ge(x0_loaded, (i * 2 + q - 1) * (2 * J0 * 16))
                    sp.sem_inc(copies_begun, 1)
                    for g in range(N1):
                        sp.wait_ge(xrep_loaded[q][g], i * 32)
                for row0, rows in ((0, F), (F, XROWS - F)):
                    for a in range(GF):
                        n = (rows - 1 - a) // GF + 1
                        dst = bass.AP(tensor=xT[q], offset=(row0 + a) * CN,
                                      ap=[[D, CB], [GF * CN, n], [1, D]])
                        sp.dma_start(dst, emb[a * CB:(a + 1) * CB, q, 0:n, :]).then_inc(xT_written[q], 16)
                sp.wait_ge(xT_written[q], (i + 1) * (2 * GF * 16))

            def load_x0(i, q):
                c = i * 2 + q
                if not isinstance(c, int):
                    sp.wait_ge(z_made, (c - 1) * GC + N0 - N1)
                elif c == 1:
                    sp.wait_ge(z_made, N0)
                for j in range(J0):
                    rows = slice(j * F, (j + 1) * F)
                    sp.dma_start(xa[rows, :], xT[q].ap()[0:F, :]).then_inc(x0_loaded, 16)
                    window = bass.AP(tensor=xT[q], offset=j * CN, ap=[[CN, F], [J0 * CN, T0], [1, CN]])
                    sp.dma_start(xb[rows, :, :], window).then_inc(x0_loaded, 16)

            def load_xrep(i, q):
                for g, n in enumerate(G1):
                    if not isinstance(i, int):
                        sp.wait_ge(z_made, first_group(2, i * 2 + q - 2) + g + 1)
                    for a in range(2):
                        src = bass.AP(tensor=xT[q], offset=(2 * G * g + a) * CN,
                                      ap=[[0, HALF], [2 * CN, n], [1, CN]])
                        sp.dma_start(xrep[a * HALF:(a + 1) * HALF, q, G * g:G * g + n, :],
                                     src).then_inc(xrep_loaded[q][g], 16)

            def load_w(dst, src, landed):
                full = (T1 - 1) * P
                sp.dma_start(dst[:, 0:T1 - 1, :], src[0:full, :].rearrange("(t p) l -> p t l", p=P)).then_inc(landed, 16)
                sp.dma_start(dst[0:HALF, T1 - 1, :], src[full:, :]).then_inc(landed, 16)

            transpose_x(0, 0)
            load_x0(0, 0)
            load_xrep(0, 0)
            load_w(w1_sb, w1, w1_in)
            load_w(w2_sb, w2, w2_in)
            transpose_x(0, 1)
            load_x0(0, 1)
            load_xrep(0, 1)
            sp.dma_start(dense_sb[:], denseT).then_inc(top_in, 16)
            sp.dma_start(wt1_sb[0:HALF, 0, :], wt1[HALF:P, :]).then_inc(top_in, 16)
            sp.dma_start(wt1_sb[HALF:P, 0, :], wt1[0:HALF, :]).then_inc(top_in, 16)
            sp.dma_start(wt1_sb[:, 1, :], wt1[P:2 * P, :]).then_inc(top_in, 16)
            sp.dma_start(wt1d_sb[:], wt1[2 * P:, :]).then_inc(top_in, 16)
            sp.dma_start(wt2_sb[:], wt2.rearrange("(k p) n -> p k n", p=P)).then_inc(top_in, 16)
            sp.dma_start(wt3_sb[:], wt3).then_inc(top_in, 16)
            sp.dma_start(bt1_sb[:], bt1).then_inc(top_in, 16)
            sp.dma_start(bt2_sb[:], bt2).then_inc(top_in, 16)
            with sp.Fori(1, PAIRS) as i:
                for q in range(2):
                    transpose_x(i, q)
                    load_x0(i, q)
                    load_xrep(i, q)
            sp.wait_ge(y_done, 1)
            sp.dma_start(out.rearrange("b o -> o b"), y_sb[:]).then_inc(y_out, 16)
            sp.wait_ge(y_out, 16)

        @block.gpsimd
        def _(pool):
            pool.wait_ge(ids_in, 32)

            def gather(i, q):
                if not isinstance(i, int):
                    pool.wait_ge(xT_written[q], i * (2 * GF * 16))
                pool.tensor_tensor(rows_sb[:, q, :], ids_sb[:, bass.ds((i * 2 + q) * NG, NG)],
                                   bases_sb[:], ALU.add).then_inc(rows_ready, 1)
                pool.wait_ge(rows_ready, i * 2 + (q + 1))
                pool.sem_inc(gathers_begun, 1)
                for g in range(NG):
                    n = min(P, (F - GF * g) * CB)
                    pool.indirect_dma_start(
                        out=emb[0:n, q, g, :], out_offset=None, in_=table,
                        in_offset=bass.IndirectOffsetOnAxis(ap=rows_sb[0:n, q, g:g + 1], axis=0),
                    ).then_inc(gathered[q], 16)

            gather(0, 0)
            gather(0, 1)
            with pool.Fori(1, PAIRS) as i:
                for q in range(2):
                    gather(i, q)

        @block.vector
        def _(dve):
            slots = cycle(range(RING))

            def products(layer, c, groups, in0, in1, loaded=None, last=False):
                rows = in0.shape[0]
                for g, n in enumerate(groups):
                    dve.wait_ge(z_free, first_group(layer, c, last) + (g + 1))
                    if loaded is not None:
                        dve.wait_ge(*loaded(g))
                    dve.tensor_tensor(z[0:rows, next(slots), 0:n, :], in0[:, G * g:G * g + n, :],
                                      in1.unsqueeze(1).to_broadcast([rows, n, CN]),
                                      ALU.mult).then_inc(z_made, 1)

            def sum_over_d(sums, direct, c, done):
                dve.tensor_reduce(sums[:, bass.ds(c * CB, CB)],
                                  direct.rearrange("p (b d) -> p b d", d=D), AX_X,
                                  ALU.add).then_inc(done, 1)

            def layer0(c):
                dve.wait_ge(x0_loaded, (c + 1) * (2 * J0 * 16))
                products(0, c, G0, xb[:], xa[:])

            def layer2_sums(c, last=False):
                dve.wait_ge(direct2_ready, c + 1)
                sum_over_d(sums2, direct2[:], c, sums2_done)

            dve.wait_ge(w0_in, 32)
            dve.tensor_tensor(w0_sb[:], w0_sb[:], w0b_sb[:], ALU.add).then_inc(w0_summed, 1)
            layer0(0)

            def pair(i, first, last):
                for q in range(2):
                    c = i * 2 + q
                    end = last and q == 1
                    dve.wait_ge(h1_ready, (c + 1) * 2)
                    products(1, c, G1, xrep[:, q], h1[:], lambda g: (xrep_loaded[q][g], (i + 1) * 32))
                    if not (first and q == 0):
                        layer2_sums(c - 1)
                    if not end:
                        layer0(c + 1)
                    dve.wait_ge(h2_ready, (c + 1) * 2)
                    products(2, c, G1, xrep[:, q], h2[:], last=end)
                    dve.wait_ge(direct01_ready, (c + 1) * 2)
                    sum_over_d(sums01, direct01[:, q], c, sums01_done)

            over_pairs(dve, pair)
            layer2_sums(CHUNKS - 1)

        @block.tensor
        def _(pe):
            pe.sem_inc(z_free, RING)
            slots = cycle(range(RING))
            banks = cycle(acc)

            def contract(layer, c, groups, w, last_rows, bank_read, last=False):
                bank = next(banks)
                if bank_read is not None:
                    pe.wait_ge(*bank_read)
                tiles = sum(groups)
                for g, n in enumerate(groups):
                    pe.wait_ge(z_made, first_group(layer, c, last) + (g + 1))
                    slot = next(slots)
                    for u in range(n):
                        t = G * g + u
                        rows = last_rows if t == tiles - 1 else w.shape[0]
                        mm = pe.matmul(bank[:], w[0:rows, t, :], z[0:rows, slot, u, :],
                                       start=(t == 0), stop=(t == tiles - 1))
                    mm.then_inc(z_free, 1)

            pe.wait_ge(w0_summed, 1)
            contract(0, 0, G0, w0_sb, R0_LAST, None)

            def pair(i, first, last):
                for q in range(2):
                    c = i * 2 + q
                    end = last and q == 1
                    if first and q == 0:
                        pe.wait_ge(w1_in, 32)
                    contract(1, c, G1, w1_sb, HALF,
                             None if first and q == 0 else (direct01_ready, c * 2 + 1))
                    if not end:
                        contract(0, c + 1, G0, w0_sb, R0_LAST,
                                 (direct01_ready, 1) if first and q == 0 else (direct2_ready, c))
                    if first and q == 0:
                        pe.wait_ge(w2_in, 32)
                    contract(2, c, G1, w2_sb, HALF,
                             (direct2_ready, c) if end else (direct01_ready, c * 2 + 2), last=end)

            over_pairs(pe, pair)

            pe.wait_ge(top_in, 9 * 16)
            pe.wait_ge(sums01_done, CHUNKS)
            pe.wait_ge(sums2_done, CHUNKS)
            for m in range(TOP // P):
                cols = slice(m * P, (m + 1) * P)
                pe.matmul(mlp_acc[m][:], wt1_sb[:, 0, cols], sums01[:], start=True, stop=False)
                pe.matmul(mlp_acc[m][:], wt1_sb[:, 1, cols], sums2[:], start=False, stop=False)
                pe.matmul(mlp_acc[m][:], wt1d_sb[:, cols], dense_sb[:], start=False,
                          stop=True).then_inc(top_done, 1)
            pe.wait_ge(direct2_ready, CHUNKS)
            for k in range(TOP // P):
                pe.wait_ge(top_relu, k + 1)
                for m in range(TOP2 // P):
                    mm = pe.matmul(acc[m][:], wt2_sb[:, k, m * P:(m + 1) * P], top1[:, k, :],
                                   start=(k == 0), stop=(k == TOP // P - 1))
                    if k == TOP // P - 1:
                        mm.then_inc(top_done, 1)
            for k in range(TOP2 // P):
                pe.wait_ge(top_relu, TOP // P + k + 1)
                mm = pe.matmul(mlp_acc[0][0:1, :], wt3_sb[:, k:k + 1], top2[:, k, :],
                               start=(k == 0), stop=(k == TOP2 // P - 1))
            mm.then_inc(top_done, 1)

        @block.scalar
        def _(act):
            lo, hi = slice(0, HALF), slice(HALF, P)
            banks = cycle(acc)

            def relu(dst, src, rows, layer):
                return act.activation(dst, src, ACT.Relu, bias=bias_sb[rows, layer:layer + 1])

            def layer0(c, q):
                bank = next(banks)
                act.wait_ge(z_free, RING + first_group(0, c) + N0)
                if not (isinstance(c, int) and c == 0):
                    act.wait_ge(z_made, first_group(1, c - 1) + N1)
                relu(h1[lo, :], bank[lo, :], lo, 0).then_inc(h1_ready, 1)
                relu(h1[hi, :], bank[lo, :], lo, 0).then_inc(h1_ready, 1)
                if not (isinstance(c, int) and c < 2):
                    act.wait_ge(sums01_done, c - 1)
                relu(direct01[hi, q, :], bank[hi, :], hi, 0).then_inc(direct01_ready, 1)

            def layer1(c, q):
                bank = next(banks)
                act.wait_ge(z_free, RING + first_group(1, c) + N1)
                if not (isinstance(c, int) and c == 0):
                    act.wait_ge(z_made, first_group(2, c - 1) + N1)
                relu(h2[lo, :], bank[lo, :], lo, 1).then_inc(h2_ready, 1)
                relu(h2[hi, :], bank[lo, :], lo, 1).then_inc(h2_ready, 1)
                relu(direct01[lo, q, :], bank[hi, :], hi, 1).then_inc(direct01_ready, 1)

            def layer2(c, last):
                bank = next(banks)
                act.wait_ge(z_free, RING + first_group(2, c, last) + N1)
                if not (isinstance(c, int) and c == 0):
                    act.wait_ge(sums2_done, c)
                relu(direct2[:], bank[:], slice(0, P), 2).then_inc(direct2_ready, 1)

            act.wait_ge(small_in, 16)
            layer0(0, 0)

            def pair(i, first, last):
                for q in range(2):
                    c = i * 2 + q
                    end = last and q == 1
                    layer1(c, q)
                    if not end:
                        layer0(c + 1, 1 - q)
                    layer2(c, end)

            over_pairs(act, pair)

            act.wait_ge(top_in, 9 * 16)
            for m in range(TOP // P):
                act.wait_ge(top_done, m + 1)
                act.activation(top1[:, m, :], mlp_acc[m][:], ACT.Relu,
                               bias=bt1_sb[:, m:m + 1]).then_inc(top_relu, 1)
            for m in range(TOP2 // P):
                act.wait_ge(top_done, TOP // P + m + 1)
                act.activation(top2[:, m, :], acc[m][:], ACT.Relu,
                               bias=bt2_sb[:, m:m + 1]).then_inc(top_relu, 1)
            act.wait_ge(top_done, TOP // P + TOP2 // P + 1)
            act.copy(y_sb[:], mlp_acc[0][0:1, :]).then_inc(y_done, 1)


def kernel(**inputs):
    import numpy as np
    import concourse.bacc as bacc
    from concourse.bass_utils import run_bass_kernel_spmd

    a = {n: np.asarray(v) for n, v in inputs.items()}
    tables = [a[f"tbl_{f}"] for f in range(F)]
    first_row = np.cumsum([0] + [t.shape[0] for t in tables[:-1]])

    ids = np.zeros((B, NG * GF), np.int32)
    ids[:, :F] = a["ids"]
    ids = ids.reshape(CHUNKS, CB, NG, GF).transpose(3, 1, 0, 2).reshape(P, CHUNKS * NG)
    bases = np.zeros(NG * GF, np.int32)
    bases[:F] = first_row
    bases = np.repeat(bases.reshape(NG, GF).T, CB, axis=0)

    w0 = a["L0_rec_W0"].reshape(F, F, L)
    w0a = np.zeros((J0, F, T0, L), w0.dtype)
    w0b = np.zeros((J0, F, T0, L), w0.dtype)
    f = np.arange(F)
    for k in range(OFFS):
        t, j = divmod(k, J0)
        w0a[j, :, t] = w0[f, (f + k) % F]
        if k:
            w0b[j, :, t] = w0[(f + k) % F, f]

    arrays = {
        "table": np.concatenate(tables, axis=0),
        "ids": ids,
        "bases": bases,
        "w0a": w0a.reshape(R0, T0, L),
        "w0b": w0b.reshape(R0, T0, L),
        "w1": a["L0_rec_W1"],
        "w2": a["L0_rec_W2"],
        "biases": np.stack([a["L0_rec_b0"], a["L0_rec_b1"], a["L0_rec_b2"]], axis=1),
        "denseT": a["dense_ctx"].T,
        "wt1": a["W_top1"],
        "bt1": a["b_top1"].reshape(TOP // P, P).T,
        "wt2": a["W_top2"],
        "bt2": a["b_top2"].reshape(TOP2 // P, P).T,
        "wt3": a["W_top3"].reshape(TOP2 // P, P).T,
    }
    arrays = {n: np.ascontiguousarray(v) for n, v in arrays.items()}
    nc = bacc.Bacc("TRN2", target_bir_lowering=False, num_devices=1)
    args = {n: nc.dram_tensor(n, v.shape, mybir.dt.from_np(v.dtype), kind="ExternalInput").ap()
            for n, v in arrays.items()}
    y = nc.dram_tensor("y", (B, 1), F32, kind="ExternalOutput").ap()
    build(nc, out=y, **args)
    r = run_bass_kernel_spmd(nc, [arrays], core_ids=[0])
    return r.results[0]["y"]
```

```python
from contextlib import ExitStack
from itertools import cycle

import concourse.bass as bass
import concourse.mybir as mybir

F32 = mybir.dt.float32
F32R = mybir.dt.float32r
I32 = mybir.dt.int32
ALU = mybir.AluOpType
ACT = mybir.ActivationFunctionType
AX_X = mybir.AxisListType.X

P = 128
F = 39
D = 16
B = 512
CB = 32
CN = CB * D
CHUNKS = B // CB
PAIRS = CHUNKS // 2
HALF = 64
L = 128
OFFS = 20
J0 = 3
R0 = J0 * F
T0 = -(-OFFS // J0)
R0_LAST = (OFFS - J0 * (T0 - 1)) * F
T1 = -(-F // 2)
G = 4
H = 2
NG1 = -(-T1 // G)
K0 = -(-T0 // H)
XROWS = 60
NG = 10
GF = P // CB
DOUBLE = 2
C_RING = 4
HL_RING = 2
HL0_RING = K0
TOP = 512
TOP2 = 256
DENSE = 16


def build(nc, table, ids, bases, w0a, w0b, w1s, w1f, w2s, w2f, biases, denseT, wt1, bt1, wt2, bt2, wt3, out):
    ctx = ExitStack()
    with ctx:
        def sb(name, shape, dt=F32):
            return ctx.enter_context(nc.sbuf_tensor(name, shape, dt))

        def bank(name):
            return ctx.enter_context(nc.psum_tensor(name, [P, CN], F32))

        def sem(name):
            return ctx.enter_context(nc.semaphore(name))

        xT = [nc.dram_tensor(f"xT{q}", [XROWS, CN], F32, kind="Internal") for q in range(2)]

        ids_sb = sb("ids_sb", [P, CHUNKS * NG], I32)
        bases_sb = sb("bases_sb", [P, NG], I32)
        rows_sb = sb("rows_sb", [P, 2, NG], I32)
        emb = sb("emb", [P, 2, NG, D])
        xa = sb("xa", [R0, CN])
        xb = sb("xb", [R0, T0, CN])
        xrep = sb("xrep", [P, NG1 + DOUBLE, G, CN])
        zf = sb("zf", [P, C_RING, H, CN])
        hl = sb("hl", [P, HL_RING, 2, H, CN], F32R)
        z0 = sb("z0", [R0, 2, H, CN])
        hl0 = sb("hl0", [R0, HL0_RING, 2, H, CN], F32R)
        w0_sb = sb("w0_sb", [R0, 2, T0, L], F32R)
        w1_sb = sb("w1_sb", [P, 2, NG1, H, L], F32R)
        w2_sb = sb("w2_sb", [P, 2, NG1, H, L], F32R)
        w1f_sb = sb("w1f_sb", [P, NG1, H, L])
        w2f_sb = sb("w2f_sb", [P, NG1, H, L])
        bias_sb = sb("bias_sb", [P, 3])
        direct01 = sb("direct01", [P, 2, CN])
        direct2 = sb("direct2", [P, CN])
        sums01 = sb("sums01", [P, B])
        sums2 = sb("sums2", [P, B])
        dense_sb = sb("dense_sb", [DENSE, B])
        wt1_sb = sb("wt1_sb", [P, 2, TOP])
        wt1d_sb = sb("wt1d_sb", [DENSE, TOP])
        wt2_sb = sb("wt2_sb", [P, TOP // P, TOP2])
        wt3_sb = sb("wt3_sb", [P, TOP2 // P])
        bt1_sb = sb("bt1_sb", [P, TOP // P])
        bt2_sb = sb("bt2_sb", [P, TOP2 // P])

        w0_in0 = z0[:, 0].rearrange("p h n -> p (h n)")[:, 0:T0 * L]
        w0_in1 = z0[:, 1].rearrange("p h n -> p (h n)")[:, 0:T0 * L]
        zf_flat = zf[:].rearrange("p r h n -> p (r h n)")
        NW = NG1 * H * L
        w1_in_sb = zf_flat[:, 0:NW]
        w2_in_sb = zf_flat[:, NW:2 * NW]
        top1 = zf_flat[:, 0:TOP // P * B].rearrange("p (m b) -> p m b", b=B)
        top2 = zf_flat[:, TOP // P * B:(TOP + TOP2) // P * B].rearrange("p (m b) -> p m b", b=B)
        y_sb = zf_flat[0:1, (TOP + TOP2) // P * B:((TOP + TOP2) // P + 1) * B]

        acc = [bank("acc0"), bank("acc1")]
        h1 = bank("h1")
        h2 = bank("h2")
        zs = ctx.enter_context(nc.psum_tensor("zs", [P, 2, H, CN], F32))

        ids_in = sem("ids_in")
        small_in = sem("small_in")
        w0_in = sem("w0_in")
        w12_in = sem("w12_in")
        top_in = sem("top_in")
        w_step = sem("w_step")
        rows_ready = sem("rows_ready")
        gathers_begun = sem("gathers_begun")
        copies_begun = sem("copies_begun")
        gathered = [sem(f"gathered{q}") for q in range(2)]
        xT_written = [sem(f"xT_written{q}") for q in range(2)]
        x0_loaded = sem("x0_loaded")
        xrep_loaded = [sem(f"xrep_loaded{g}") for g in range(NG1 + DOUBLE)]
        zf_made = sem("zf_made")
        zf_free = sem("zf_free")
        zs_made = sem("zs_made")
        hi_made = sem("hi_made")
        lo_made = sem("lo_made")
        hl_free = sem("hl_free")
        z0_made = sem("z0_made")
        hi0_made = sem("hi0_made")
        lo0_made = sem("lo0_made")
        hl0_free = sem("hl0_free")
        h1_ready = sem("h1_ready")
        h2_ready = sem("h2_ready")
        direct01_ready = sem("direct01_ready")
        direct2_ready = sem("direct2_ready")
        sums01_done = sem("sums01_done")
        sums2_done = sem("sums2_done")
        top_done = sem("top_done")
        top_relu = sem("top_relu")
        y_done = sem("y_done")
        y_out = sem("y_out")

        block = ctx.enter_context(nc.Block())

        def group(layer, c, g):
            return c * (2 * NG1) + ((layer - 1) * NG1 + g)

        def over_pairs(eng, pair):
            pair(0, True, False)
            with eng.Fori(1, PAIRS - 1) as i:
                pair(i, False, False)
            pair(PAIRS - 1, False, True)

        def known(c, *values):
            return isinstance(c, int) and c in values

        def xrep_slot(q, g):
            return q * DOUBLE + g if g < DOUBLE else g + DOUBLE

        def tiles0(k):
            return min(H, T0 - H * k)

        def product0(eng, k):
            n = tiles0(k)
            eng.tensor_tensor(z0[:, k % 2, 0:n, :], xb[:, H * k:H * k + n, :],
                              xa[:].unsqueeze(1).to_broadcast([R0, n, CN]), ALU.mult).then_inc(z0_made, 1)

        def rest0(eng, c, k):
            n = tiles0(k)
            eng.wait_ge(hi0_made, c * K0 + (k + 1))
            eng.tensor_tensor(hl0[:, k, 1, 0:n, :], z0[:, k % 2, 0:n, :], hl0[:, k, 0, 0:n, :].bitcast(F32),
                              ALU.subtract).then_inc(lo0_made, 1)

        @block.sync
        def _(sp):
            sp.dma_start(ids_sb[:], ids).then_inc(ids_in, 16)
            sp.dma_start(bases_sb[:], bases).then_inc(ids_in, 16)
            sp.dma_start(bias_sb[:], biases).then_inc(small_in, 16)
            sp.dma_start(w0_in0, w0a.rearrange("p t l -> p (t l)")).then_inc(w0_in, 16)
            sp.dma_start(w0_in1, w0b.rearrange("p t l -> p (t l)")).then_inc(w0_in, 16)
            sp.dma_start(w1_in_sb, w1s).then_inc(w12_in, 16)
            sp.dma_start(w2_in_sb, w2s).then_inc(w12_in, 16)
            sp.dma_start(w1f_sb[:].rearrange("p g h l -> p (g h l)"), w1f).then_inc(w12_in, 16)
            sp.dma_start(w2f_sb[:].rearrange("p g h l -> p (g h l)"), w2f).then_inc(w12_in, 16)

            def transpose_x(i, q):
                sp.wait_ge(gathered[q], (i + 1) * (NG * 16))
                sp.sem_inc(copies_begun, 1)
                if not known(i, 0):
                    sp.wait_ge(x0_loaded, (i * 2 + q - 1) * (2 * J0 * 16))
                    sp.sem_inc(copies_begun, 1)
                    for g in range(NG1):
                        sp.wait_ge(xrep_loaded[xrep_slot(q, g)], (i if g < DOUBLE else i * 2 + q - 1) * 32)
                        sp.sem_inc(copies_begun, 1)
                for row0, rows in ((0, F), (F, XROWS - F)):
                    for a in range(GF):
                        n = (rows - 1 - a) // GF + 1
                        dst = bass.AP(tensor=xT[q], offset=(row0 + a) * CN,
                                      ap=[[D, CB], [GF * CN, n], [1, D]])
                        sp.dma_start(dst, emb[a * CB:(a + 1) * CB, q, 0:n, :]).then_inc(xT_written[q], 16)
                sp.wait_ge(xT_written[q], (i + 1) * (2 * GF * 16))
                sp.sem_inc(copies_begun, 1)

            def load_x0(i, q):
                c = i * 2 + q
                if not known(c, 0):
                    sp.wait_ge(z0_made, c * K0)
                for j in range(J0):
                    rows = slice(j * F, (j + 1) * F)
                    sp.dma_start(xa[rows, :], xT[q].ap()[0:F, :]).then_inc(x0_loaded, 16)
                    window = bass.AP(tensor=xT[q], offset=j * CN, ap=[[CN, F], [J0 * CN, T0], [1, CN]])
                    sp.dma_start(xb[rows, :, :], window).then_inc(x0_loaded, 16)

            def load_xrep(i, q, groups):
                c = i * 2 + q
                for g in groups:
                    back = 2 if g < DOUBLE else 1
                    if not (isinstance(c, int) and c < back):
                        sp.wait_ge(zs_made, group(2, c - back, g + 1))
                    for a in range(2):
                        src = bass.AP(tensor=xT[q], offset=(2 * G * g + a) * CN,
                                      ap=[[0, HALF], [2 * CN, G], [1, CN]])
                        slot = xrep_slot(q, g)
                        sp.dma_start(xrep[a * HALF:(a + 1) * HALF, slot, :, :], src).then_inc(xrep_loaded[slot], 16)

            early, late = range(DOUBLE), range(DOUBLE, NG1)
            transpose_x(0, 0)
            load_x0(0, 0)
            load_xrep(0, 0, range(NG1))
            transpose_x(0, 1)
            load_x0(0, 1)
            sp.dma_start(dense_sb[:], denseT).then_inc(top_in, 16)
            sp.dma_start(wt1_sb[0:HALF, 0, :], wt1[HALF:P, :]).then_inc(top_in, 16)
            sp.dma_start(wt1_sb[HALF:P, 0, :], wt1[0:HALF, :]).then_inc(top_in, 16)
            sp.dma_start(wt1_sb[:, 1, :], wt1[P:2 * P, :]).then_inc(top_in, 16)
            sp.dma_start(wt1d_sb[:], wt1[2 * P:, :]).then_inc(top_in, 16)
            sp.dma_start(wt2_sb[:], wt2.rearrange("(k p) n -> p k n", p=P)).then_inc(top_in, 16)
            sp.dma_start(wt3_sb[:], wt3).then_inc(top_in, 16)
            sp.dma_start(bt1_sb[:], bt1).then_inc(top_in, 16)
            sp.dma_start(bt2_sb[:], bt2).then_inc(top_in, 16)

            def pair(i, first, last):
                for q in range(2):
                    if last and q == 1:
                        break
                    i1, q1 = (i, 1) if q == 0 else (i + 1, 0)
                    load_xrep(i1, q1, early)
                    if not last:
                        transpose_x(i + 1, q)
                        load_x0(i + 1, q)
                    load_xrep(i1, q1, late)

            over_pairs(sp, pair)
            sp.wait_ge(y_done, 1)
            sp.dma_start(out.rearrange("b o -> o b"), y_sb).then_inc(y_out, 16)
            sp.wait_ge(y_out, 16)

        @block.gpsimd
        def _(pool):
            def gather(i, q):
                if not known(i, 0):
                    pool.wait_ge(xT_written[q], i * (2 * GF * 16))
                pool.tensor_tensor(rows_sb[:, q, :], ids_sb[:, bass.ds((i * 2 + q) * NG, NG)],
                                   bases_sb[:], ALU.add).then_inc(rows_ready, 1)
                pool.wait_ge(rows_ready, i * 2 + (q + 1))
                pool.sem_inc(gathers_begun, 1)
                for g in range(NG):
                    n = min(P, (F - GF * g) * CB)
                    pool.indirect_dma_start(
                        out=emb[0:n, q, g, :], out_offset=None, in_=table,
                        in_offset=bass.IndirectOffsetOnAxis(ap=rows_sb[0:n, q, g:g + 1], axis=0),
                    ).then_inc(gathered[q], 16)

            def layer0(i, q):
                c = i * 2 + q
                pool.wait_ge(x0_loaded, (c + 1) * (2 * J0 * 16))
                for k in range(K0):
                    pool.wait_ge(lo0_made, c * K0 + k - 1)
                    product0(pool, k)
                    if k:
                        rest0(pool, c, k - 1)
                rest0(pool, c, K0 - 1)

            pool.wait_ge(ids_in, 32)
            gather(0, 0)
            gather(0, 1)

            def pair(i, first, last):
                for q in range(2):
                    if not (first and q == 0):
                        layer0(i, q)
                    if not last:
                        gather(i + 1, q)

            over_pairs(pool, pair)

        @block.vector
        def _(dve):
            h_of = {1: h1, 2: h2}

            def products(dst, layer, c, q, g, half, made):
                in0 = xrep[:, xrep_slot(q, g), half * H:(half + 1) * H, :]
                dve.tensor_tensor(dst, in0, h_of[layer][:].unsqueeze(1).to_broadcast([P, H, CN]),
                                  ALU.mult).then_inc(made, 1)

            def group_products(layer, c, q, g):
                at = group(layer, c, g)
                dve.wait_ge(zf_free, at + 1)
                products(zf[:, g_of[0] % C_RING], layer, c, q, g, 1, zf_made)
                if not (isinstance(at, int) and at < 2):
                    dve.wait_ge(lo_made, at - 1)
                products(zs[:, g_of[0] % 2], layer, c, q, g, 0, zs_made)
                g_of[0] += 1

            def group_rest(layer, c, g, back):
                n = g_of[0] - 1 - back
                dve.wait_ge(hi_made, group(layer, c, g) + 1)
                dve.tensor_tensor(hl[:, n % HL_RING, 1], zs[:, n % 2], hl[:, n % HL_RING, 0].bitcast(F32),
                                  ALU.subtract).then_inc(lo_made, 1)

            def sum_over_d(sums, direct, c, done):
                dve.tensor_reduce(sums[:, bass.ds(c * CB, CB)],
                                  direct.rearrange("p (b d) -> p b d", d=D), AX_X,
                                  ALU.add).then_inc(done, 1)

            def layer2_sums(c):
                dve.wait_ge(direct2_ready, c + 1)
                sum_over_d(sums2, direct2[:], c, sums2_done)

            def layer01_sums(c, q):
                dve.wait_ge(direct01_ready, (c + 1) * 2)
                sum_over_d(sums01, direct01[:, q], c, sums01_done)

            def split_weights(dst, src, step):
                hi, lo = dst
                dve.tensor_copy(hi, src).then_inc(w_step, 1)
                dve.wait_ge(w_step, step + 1)
                dve.tensor_tensor(lo, src, hi.bitcast(F32), ALU.subtract).then_inc(w_step, 1)

            dve.wait_ge(w0_in, 32)
            dve.tensor_tensor(w0_in0, w0_in0, w0_in1, ALU.add).then_inc(w_step, 1)
            dve.wait_ge(w_step, 1)
            flat0 = [w0_sb[:, s].rearrange("p t l -> p (t l)") for s in range(2)]
            split_weights(flat0, w0_in0, 1)
            def chunk0_layer0():
                dve.wait_ge(x0_loaded, 2 * J0 * 16)
                dve.wait_ge(w_step, 7)
                product0(dve, 0)
                product0(dve, 1)
                for k in range(K0):
                    rest0(dve, 0, k)
                    if k + 2 < K0:
                        dve.wait_ge(lo0_made, k + 1)
                        product0(dve, k + 2)

            dve.wait_ge(w12_in, 64)
            for n, (w, src) in enumerate(((w1_sb, w1_in_sb), (w2_sb, w2_in_sb))):
                split_weights([w[:, s].rearrange("p g h l -> p (g h l)") for s in range(2)], src, 3 + 2 * n)
            chunk0_layer0()
            g_of = [0]

            def pair(i, first, last):
                for q in range(2):
                    c = i * 2 + q
                    dve.wait_ge(h1_ready, (c + 1) * 2)
                    for g in range(NG1):
                        dve.wait_ge(xrep_loaded[xrep_slot(q, g)], (i + 1 if g < DOUBLE else c + 1) * 32)
                        group_products(1, c, q, g)
                        if g:
                            group_rest(1, c, g - 1, 1)
                    group_rest(1, c, NG1 - 1, 0)
                    if not (first and q == 0):
                        layer2_sums(c - 1)
                        layer01_sums(c - 1, 1 - q)
                    dve.wait_ge(h2_ready, (c + 1) * 2)
                    for g in range(NG1):
                        group_products(2, c, q, g)
                        if g:
                            group_rest(2, c, g - 1, 1)
                    group_rest(2, c, NG1 - 1, 0)

            over_pairs(dve, pair)
            layer01_sums(CHUNKS - 1, 1)
            layer2_sums(CHUNKS - 1)

        @block.tensor
        def _(pe):
            pe.sem_inc(zf_free, C_RING)
            pe.sem_inc(hl_free, HL_RING)
            pe.sem_inc(hl0_free, HL0_RING)
            banks = cycle(acc)
            g_of = [0]

            def layer0(c, bank_read):
                bank = next(banks)
                if bank_read is not None:
                    pe.wait_ge(*bank_read)
                for k in range(K0):
                    n = tiles0(k)
                    pe.wait_ge(hi0_made, c * K0 + (k + 1))
                    for part_w, part_z in ((1, 0), (0, 0), (0, 1)):
                        if part_z:
                            pe.wait_ge(lo0_made, c * K0 + (k + 1))
                        for u in range(n):
                            t = H * k + u
                            rows = R0_LAST if t == T0 - 1 else R0
                            mm = pe.matmul(bank[:], w0_sb[0:rows, part_w, t, :], hl0[0:rows, k, part_z, u, :],
                                           start=(t == 0 and part_w == 1),
                                           stop=(t == T0 - 1 and part_z == 1))
                    mm.then_inc(hl0_free, 1)

            def layer12(layer, c, bank_read):
                w, wf = ((w1_sb, w1f_sb), (w2_sb, w2f_sb))[layer - 1]
                bank = next(banks)
                pe.wait_ge(*bank_read)
                def split_pass(g, back, part_w, part_z):
                    slot = (g_of[0] - 1 - back) % HL_RING
                    for u in range(H):
                        mm = pe.matmul(bank[:], w[:, part_w, g, u, :], hl[:, slot, part_z, u, :],
                                       start=False, stop=(g == NG1 - 1 and u == H - 1 and part_z == 1))
                    return mm

                def rest_pass(g, back):
                    pe.wait_ge(lo_made, group(layer, c, g) + 1)
                    split_pass(g, back, 0, 1).then_inc(hl_free, 1)

                for g in range(NG1):
                    at = group(layer, c, g)
                    pe.wait_ge(zf_made, at + 1)
                    for u in range(H):
                        rows = HALF if g == NG1 - 1 and u == H - 1 else P
                        mm = pe.matmul(bank[:], wf[0:rows, g, u, :], zf[0:rows, g_of[0] % C_RING, u, :],
                                       start=(g == 0 and u == 0), stop=False)
                    mm.then_inc(zf_free, 1)
                    g_of[0] += 1
                    pe.wait_ge(hi_made, at + 1)
                    split_pass(g, 0, 1, 0)
                    split_pass(g, 0, 0, 0)
                    if g:
                        rest_pass(g - 1, 1)
                rest_pass(NG1 - 1, 0)

            pe.wait_ge(w_step, 7)
            layer0(0, None)

            def pair(i, first, last):
                for q in range(2):
                    c = i * 2 + q
                    end = last and q == 1
                    layer12(1, c, (w12_in, 64) if first and q == 0 else (direct01_ready, c * 2 + 1))
                    if not end:
                        layer0(c + 1, (direct01_ready, 1) if first and q == 0 else (direct2_ready, c))
                    layer12(2, c, (direct2_ready, c) if end else (direct01_ready, c * 2 + 2))

            over_pairs(pe, pair)

            pe.wait_ge(top_in, 9 * 16)
            pe.wait_ge(sums01_done, CHUNKS)
            pe.wait_ge(sums2_done, CHUNKS)
            for m in range(TOP // P):
                cols = slice(m * P, (m + 1) * P)
                pe.matmul(zs[:, m // 2, m % 2, :], wt1_sb[:, 0, cols], sums01[:], start=True, stop=False)
                pe.matmul(zs[:, m // 2, m % 2, :], wt1_sb[:, 1, cols], sums2[:], start=False, stop=False)
                pe.matmul(zs[:, m // 2, m % 2, :], wt1d_sb[:, cols], dense_sb[:], start=False,
                          stop=True).then_inc(top_done, 1)
            pe.wait_ge(direct2_ready, CHUNKS)
            for k in range(TOP // P):
                pe.wait_ge(top_relu, k + 1)
                for m in range(TOP2 // P):
                    mm = pe.matmul(acc[m][:], wt2_sb[:, k, m * P:(m + 1) * P], top1[:, k, :],
                                   start=(k == 0), stop=(k == TOP // P - 1))
                    if k == TOP // P - 1:
                        mm.then_inc(top_done, 1)
            for k in range(TOP2 // P):
                pe.wait_ge(top_relu, TOP // P + k + 1)
                mm = pe.matmul(zs[0:1, 0, 0, :], wt3_sb[:, k:k + 1], top2[:, k, :],
                               start=(k == 0), stop=(k == TOP2 // P - 1))
            mm.then_inc(top_done, 1)

        @block.scalar
        def _(act):
            lo, hi = slice(0, HALF), slice(HALF, P)
            banks = cycle(acc)
            g_of = [0]

            def relu(dst, src, rows, layer):
                return act.activation(dst, src, ACT.Relu, bias=bias_sb[rows, layer:layer + 1])

            def split0(c, k):
                n = tiles0(k)
                act.wait_ge(hl0_free, c * K0 + (k + 1))
                act.wait_ge(z0_made, c * K0 + (k + 1))
                act.copy(hl0[:, k, 0, 0:n, :], z0[:, k % 2, 0:n, :]).then_inc(hi0_made, 1)

            def split12(layer, c, g):
                at = group(layer, c, g)
                act.wait_ge(hl_free, at + 1)
                act.wait_ge(zs_made, at + 1)
                act.copy(hl[:, g_of[0] % HL_RING, 0], zs[:, g_of[0] % 2]).then_inc(hi_made, 1)
                g_of[0] += 1

            def layer0(c, q):
                bank = next(banks)
                act.wait_ge(hl0_free, HL0_RING + (c + 1) * K0)
                if not known(c, 0):
                    act.wait_ge(zs_made, group(1, c - 1, NG1))
                relu(h1[lo, :], bank[lo, :], lo, 0).then_inc(h1_ready, 1)
                relu(h1[hi, :], bank[lo, :], lo, 0).then_inc(h1_ready, 1)
                if not known(c, 0, 1):
                    act.wait_ge(sums01_done, c - 1)
                relu(direct01[hi, q, :], bank[hi, :], hi, 0).then_inc(direct01_ready, 1)

            def layer1(c, q):
                bank = next(banks)
                act.wait_ge(hl_free, group(1, c, NG1) + HL_RING)
                if not known(c, 0):
                    act.wait_ge(zs_made, group(2, c - 1, NG1))
                relu(h2[lo, :], bank[lo, :], lo, 1).then_inc(h2_ready, 1)
                relu(h2[hi, :], bank[lo, :], lo, 1).then_inc(h2_ready, 1)
                relu(direct01[lo, q, :], bank[hi, :], hi, 1).then_inc(direct01_ready, 1)

            def layer2(c, bank):
                act.wait_ge(hl_free, group(2, c, NG1) + HL_RING)
                if not known(c, 0):
                    act.wait_ge(sums2_done, c)
                relu(direct2[:], bank[:], slice(0, P), 2).then_inc(direct2_ready, 1)

            act.wait_ge(small_in, 16)
            for k in range(K0):
                split0(0, k)
            layer0(0, 0)
            split0(1, 0)
            split0(1, 1)
            layer2_bank = [None]

            def pair(i, first, last):
                for q in range(2):
                    c = i * 2 + q
                    end = last and q == 1
                    for g in range(NG1):
                        split12(1, c, g)
                        if g in (1, 3) and not end:
                            split0(c + 1, 2 + g // 2)
                        if g == 3 and not (first and q == 0):
                            layer2(c - 1, layer2_bank[0])
                    layer1(c, q)
                    for g in range(NG1):
                        split12(2, c, g)
                        if g == 2 and not end:
                            layer0(c + 1, 1 - q)
                        if g in (2, 4) and not last:
                            split0(c + 2, g // 2 - 1)
                    layer2_bank[0] = next(banks)

            over_pairs(act, pair)
            layer2(CHUNKS - 1, layer2_bank[0])

            act.wait_ge(top_in, 9 * 16)
            for m in range(TOP // P):
                act.wait_ge(top_done, m + 1)
                act.activation(top1[:, m, :], zs[:, m // 2, m % 2, :], ACT.Relu,
                               bias=bt1_sb[:, m:m + 1]).then_inc(top_relu, 1)
            for m in range(TOP2 // P):
                act.wait_ge(top_done, TOP // P + m + 1)
                act.activation(top2[:, m, :], acc[m][:], ACT.Relu,
                               bias=bt2_sb[:, m:m + 1]).then_inc(top_relu, 1)
            act.wait_ge(top_done, TOP // P + TOP2 // P + 1)
            act.copy(y_sb, zs[0:1, 0, 0, :]).then_inc(y_done, 1)


def kernel(**inputs):
    import numpy as np
    import concourse.bacc as bacc
    from concourse.bass_utils import run_bass_kernel_spmd

    a = {n: np.asarray(v) for n, v in inputs.items()}
    tables = [a[f"tbl_{f}"] for f in range(F)]
    first_row = np.cumsum([0] + [t.shape[0] for t in tables[:-1]])

    ids = np.zeros((B, NG * GF), np.int32)
    ids[:, :F] = a["ids"]
    ids = ids.reshape(CHUNKS, CB, NG, GF).transpose(3, 1, 0, 2).reshape(P, CHUNKS * NG)
    bases = np.zeros(NG * GF, np.int32)
    bases[:F] = first_row
    bases = np.repeat(bases.reshape(NG, GF).T, CB, axis=0)

    w0 = a["L0_rec_W0"].reshape(F, F, L)
    w0a = np.zeros((J0, F, T0, L), w0.dtype)
    w0b = np.zeros((J0, F, T0, L), w0.dtype)
    f = np.arange(F)
    for k in range(OFFS):
        t, j = divmod(k, J0)
        w0a[j, :, t] = w0[f, (f + k) % F]
        if k:
            w0b[j, :, t] = w0[(f + k) % F, f]

    w12 = []
    for name in ("L0_rec_W1", "L0_rec_W2"):
        w = np.zeros((NG1 * G * P, L), a[name].dtype)
        w[:F * HALF] = a[name]
        w = w.reshape(NG1, 2, H, P, L).transpose(1, 3, 0, 2, 4).reshape(2, P, NG1 * H * L)
        w12.append((w[0], w[1]))

    arrays = {
        "table": np.concatenate(tables, axis=0),
        "ids": ids,
        "bases": bases,
        "w0a": w0a.reshape(R0, T0, L),
        "w0b": w0b.reshape(R0, T0, L),
        "w1s": w12[0][0],
        "w1f": w12[0][1],
        "w2s": w12[1][0],
        "w2f": w12[1][1],
        "biases": np.stack([a["L0_rec_b0"], a["L0_rec_b1"], a["L0_rec_b2"]], axis=1),
        "denseT": a["dense_ctx"].T,
        "wt1": a["W_top1"],
        "bt1": a["b_top1"].reshape(TOP // P, P).T,
        "wt2": a["W_top2"],
        "bt2": a["b_top2"].reshape(TOP2 // P, P).T,
        "wt3": a["W_top3"].reshape(TOP2 // P, P).T,
    }
    arrays = {n: np.ascontiguousarray(v) for n, v in arrays.items()}
    nc = bacc.Bacc("TRN2", target_bir_lowering=False, num_devices=1)
    args = {n: nc.dram_tensor(n, v.shape, mybir.dt.from_np(v.dtype), kind="ExternalInput").ap()
            for n, v in arrays.items()}
    y = nc.dram_tensor("y", (B, 1), F32, kind="ExternalOutput").ap()
    build(nc, out=y, **args)
    r = run_bass_kernel_spmd(nc, [arrays], core_ids=[0])
    return r.results[0]["y"]
```

```python
from contextlib import ExitStack
from itertools import cycle

import concourse.bass as bass
import concourse.mybir as mybir

F32 = mybir.dt.float32
F32R = mybir.dt.float32r
I32 = mybir.dt.int32
ALU = mybir.AluOpType
ACT = mybir.ActivationFunctionType
AX_X = mybir.AxisListType.X

P = 128
F = 39
D = 16
B = 512
CB = 32
CN = CB * D
CHUNKS = B // CB
PAIRS = CHUNKS // 2
HALF = 64
L = 128
OFFS = 20
J0 = 3
R0 = J0 * F
T0 = -(-OFFS // J0)
R0_LAST = (OFFS - J0 * (T0 - 1)) * F
T1 = -(-F // 2)
G = 4
H = 2
NG1 = -(-T1 // G)
K0 = -(-T0 // H)
XROWS = 59
NG = 10
GF = P // CB
DOUBLE = 2
C_RING = 4
HL_RING = 2
BY_POOL = {1: (1,), 2: (1, 3)}
POOLS = sum(len(g) for g in BY_POOL.values())
SPLITS = 2 * NG1 - POOLS
TOP = 512
TOP2 = 256
DENSE = 16


def build(nc, table, ids, bases, w0a, w0b, w1s, w1f, w2s, w2f, biases, denseT, wt1, bt1, wt2, bt2, wt3, out):
    ctx = ExitStack()
    with ctx:
        def sb(name, shape, dt=F32):
            return ctx.enter_context(nc.sbuf_tensor(name, shape, dt))

        def bank(name):
            return ctx.enter_context(nc.psum_tensor(name, [P, CN], F32))

        def sem(name):
            return ctx.enter_context(nc.semaphore(name))

        xT = [nc.dram_tensor(f"xT{q}", [XROWS, CN], F32, kind="Internal") for q in range(2)]
        pre_dram = nc.dram_tensor("pre_dram", [P, TOP // P * B], F32, kind="Internal")

        ids_sb = sb("ids_sb", [P, CHUNKS * NG], I32)
        bases_sb = sb("bases_sb", [P, NG], I32)
        rows_sb = sb("rows_sb", [P, 2, NG], I32)
        emb = sb("emb", [P, 2, NG, D])
        xa = sb("xa", [R0, CN])
        xb = sb("xb", [R0, T0, CN])
        xrep = sb("xrep", [P, NG1 + DOUBLE, G, CN])
        zf = sb("zf", [P, C_RING, H, CN])
        hl = sb("hl", [P, HL_RING, 2, H, CN], F32R)
        z0 = sb("z0", [R0, 2, H, CN])
        hl0 = sb("hl0", [R0, K0, 2, H, CN], F32R)
        zb = sb("zb", [P, H, CN])
        hlb = sb("hlb", [P, 2, H, CN], F32R)
        w0_sb = sb("w0_sb", [R0, 2, T0, L], F32R)
        w1_sb = sb("w1_sb", [P, 2, NG1, H, L], F32R)
        w2_sb = sb("w2_sb", [P, 2, NG1, H, L], F32R)
        w1f_sb = sb("w1f_sb", [P, NG1, H, L])
        w2f_sb = sb("w2f_sb", [P, NG1, H, L])
        bias_sb = sb("bias_sb", [P, 3])
        direct01 = sb("direct01", [P, 2, CN])
        direct2 = sb("direct2", [P, CN])
        sums01 = sb("sums01", [P, B])
        sums2 = sb("sums2", [P, B])
        wt3_sb = sb("wt3_sb", [P, TOP2 // P])
        bt1_sb = sb("bt1_sb", [P, TOP // P])
        bt2_sb = sb("bt2_sb", [P, TOP2 // P])

        zf_flat = zf[:].rearrange("p r h n -> p (r h n)")
        NW = NG1 * H * L
        w1_in_sb = zf_flat[:, 0:NW]
        w2_in_sb = zf_flat[:, NW:2 * NW]
        w0f = zf_flat[0:R0, 2 * NW:2 * NW + T0 * L]
        w0_in1 = z0[:, 1].rearrange("p h n -> p (h n)")[:, 0:T0 * L]
        w0f_tiles = w0f.rearrange("p (t l) -> p t l", l=L)
        z_first = [z0[:, 0], z0[:, 1], zb[0:R0], zf[0:R0, 0]]
        xr = [xrep[:, n].rearrange("p g n -> p (g n)") for n in range(DOUBLE)]
        wt1_sb = xr[0][:, 0:2 * TOP].rearrange("p (k m) -> p k m", m=TOP)
        wt2_sb = xr[0][:, 2 * TOP:2 * TOP + TOP // P * TOP2].rearrange("p (k m) -> p k m", m=TOP2)
        pre_sb = xr[1].rearrange("p (m b) -> p m b", b=B)
        xr1 = [xrep[:, DOUBLE + n].rearrange("p g n -> p (g n)") for n in range(DOUBLE)]
        pre_first = xr1[0].rearrange("p (m b) -> p m b", b=B)
        wt1d_sb = xr1[1][0:DENSE, 0:TOP]
        dense_sb = xr1[1][0:DENSE, TOP:TOP + B]
        top1 = zf_flat[:, 0:TOP // P * B].rearrange("p (m b) -> p m b", b=B)
        top2 = zf_flat[:, TOP // P * B:(TOP + TOP2) // P * B].rearrange("p (m b) -> p m b", b=B)
        y_sb = zf_flat[0:1, (TOP + TOP2) // P * B:((TOP + TOP2) // P + 1) * B]

        w_whole = [w0f, w1_in_sb, w2_in_sb]
        w_parts = [[w0_sb[:, s].rearrange("p t l -> p (t l)") for s in range(2)]]
        w_parts += [[w[:, s].rearrange("p g h l -> p (g h l)") for s in range(2)] for w in (w1_sb, w2_sb)]

        acc = [bank("acc0"), bank("acc1")]
        h1 = bank("h1")
        h2 = bank("h2")
        zs = ctx.enter_context(nc.psum_tensor("zs", [P, 2, H, CN], F32))

        top_banks = [h1, acc[1], zs[:, 0, 0, :], zs[:, 0, 1, :]]

        ids_in = sem("ids_in")
        small_in = sem("small_in")
        w0_in = sem("w0_in")
        w12_in = sem("w12_in")
        top_in = sem("top_in")
        dense_in = sem("dense_in")
        dense_done = sem("dense_done")
        pre_left = sem("pre_left")
        pre_stored = sem("pre_stored")
        top_sum = sem("top_sum")
        top_small_in = sem("top_small_in")
        w_step = sem("w_step")
        w_hi = sem("w_hi")
        rows_ready = sem("rows_ready")
        gathers_begun = sem("gathers_begun")
        copies_begun = sem("copies_begun")
        gathered = [sem(f"gathered{q}") for q in range(2)]
        xT_written = [sem(f"xT_written{q}") for q in range(2)]
        x0_loaded = sem("x0_loaded")
        x0_first = [sem("x0_first0"), sem("x0_first1")]
        xrep_loaded = [sem(f"xrep_loaded{g}") for g in range(NG1 + DOUBLE)]
        zf_made = sem("zf_made")
        zf_free = sem("zf_free")
        zs_made = sem("zs_made")
        hi_made = sem("hi_made")
        lo_made = sem("lo_made")
        hl_free = sem("hl_free")
        z00_made = sem("z00_made")
        z0_made = sem("z0_made")
        hi0_made = sem("hi0_made")
        lo0_made = sem("lo0_made")
        hl0_free = sem("hl0_free")
        zb_made = sem("zb_made")
        hib_made = sem("hib_made")
        lob_made = sem("lob_made")
        hlb_free = sem("hlb_free")
        h1_ready = sem("h1_ready")
        h2_ready = sem("h2_ready")
        direct01_ready = sem("direct01_ready")
        direct2_ready = sem("direct2_ready")
        sums01_done = sem("sums01_done")
        sums2_done = sem("sums2_done")
        top_done = sem("top_done")
        top_relu = sem("top_relu")
        y_done = sem("y_done")
        y_out = sem("y_out")

        block = ctx.enter_context(nc.Block())

        def group(layer, c, g):
            return c * (2 * NG1) + ((layer - 1) * NG1 + g)

        def pools_before(layer, g):
            return (len(BY_POOL[1]) if layer == 2 else 0) + sum(1 for b in BY_POOL[layer] if b < g)

        def split_group(layer, c, g):
            return c * SPLITS + ((layer - 1) * NG1 + g - pools_before(layer, g))

        def pool_group(layer, c, g):
            return c * POOLS + pools_before(layer, g)

        def over_pairs(eng, pair):
            pair(0, True, False)
            with eng.Fori(1, PAIRS - 1) as i:
                pair(i, False, False)
            pair(PAIRS - 1, False, True)

        def split_half(g):
            return 1 if g == NG1 - 1 else 0

        def xrep_loads(g):
            return 3 if g == NG1 - 1 else 2

        def known(c, *values):
            return isinstance(c, int) and c in values

        def xrep_slot(q, g):
            return q * DOUBLE + g if g < DOUBLE else g + DOUBLE

        def tiles0(k):
            return min(H, T0 - H * k)

        def product0(eng, k, dst):
            n = tiles0(k)
            made = z0_made if k else z00_made
            eng.tensor_tensor(dst[:, 0:n, :], xb[:, H * k:H * k + n, :],
                              xa[:].unsqueeze(1).to_broadcast([R0, n, CN]), ALU.mult).then_inc(made, 1)

        def rest0(eng, c, k):
            n = tiles0(k)
            eng.wait_ge(hi0_made, (c - 1) * K0 + (k + 1))
            eng.tensor_tensor(hl0[:, k, 1, 0:n, :], z0[:, k % 2, 0:n, :], hl0[:, k, 0, 0:n, :].bitcast(F32),
                              ALU.subtract).then_inc(lo0_made, 1)

        @block.sync
        def _(sp):
            sp.dma_start(ids_sb[:], ids).then_inc(ids_in, 16)
            sp.dma_start(bases_sb[:], bases).then_inc(ids_in, 16)
            sp.dma_start(bias_sb[:], biases).then_inc(small_in, 16)
            sp.dma_start(w0f, w0a.rearrange("p t l -> p (t l)")).then_inc(w0_in, 16)
            sp.dma_start(w0_in1, w0b.rearrange("p t l -> p (t l)")).then_inc(w0_in, 16)
            sp.dma_start(wt1d_sb, wt1[2 * P:, :]).then_inc(dense_in, 16)
            sp.dma_start(dense_sb, denseT).then_inc(dense_in, 16)
            sp.dma_start(w1_in_sb, w1s).then_inc(w12_in, 16)
            sp.dma_start(w2_in_sb, w2s).then_inc(w12_in, 16)
            sp.dma_start(w1f_sb[:].rearrange("p g h l -> p (g h l)"), w1f).then_inc(w12_in, 16)
            sp.dma_start(w2f_sb[:].rearrange("p g h l -> p (g h l)"), w2f).then_inc(w12_in, 16)
            sp.dma_start(wt3_sb[:], wt3).then_inc(top_small_in, 16)
            sp.dma_start(bt1_sb[:], bt1).then_inc(top_small_in, 16)
            sp.dma_start(bt2_sb[:], bt2).then_inc(top_small_in, 16)

            def transpose_x(i, q, meanwhile=None):
                sp.wait_ge(gathered[q], (i + 1) * (NG * 16))
                sp.sem_inc(copies_begun, 1)
                if not known(i, 0):
                    sp.wait_ge(x0_loaded, (i * 2 + q - 1) * (2 * J0 * 16))
                    sp.sem_inc(copies_begun, 1)
                    for g in range(NG1):
                        sp.wait_ge(xrep_loaded[xrep_slot(q, g)],
                                   (i if g < DOUBLE else i * 2 + q - 1) * (xrep_loads(g) * 16))
                        sp.sem_inc(copies_begun, 1)
                for row0, n0, n1, parts in ((0, 0, NG - 1, P), (0, NG - 1, NG, (F - GF * (NG - 1)) * CB),
                                            (F, 0, (XROWS - F) // GF, P)):
                    dst = bass.AP(tensor=xT[q], offset=(row0 + GF * n0) * CN,
                                  ap=[[D, parts], [GF * CN, n1 - n0], [1, D]])
                    sp.dma_start(dst, emb[0:parts, q, n0:n1, :]).then_inc(xT_written[q], 16)
                if meanwhile is not None:
                    meanwhile()
                sp.wait_ge(xT_written[q], (i + 1) * (3 * 16))
                sp.sem_inc(copies_begun, 1)

            def load_first_x0():
                rows = [slice(j * F, (j + 1) * F) for j in range(J0)]
                for j in range(J0):
                    sp.dma_start(xa[rows[j], :], xT[0].ap()[0:F, :]).then_inc(x0_first[0], 16)
                for t0, t1, loaded in ((0, H, x0_first[0]), (H, 2 * H, x0_first[1]), (2 * H, T0, x0_loaded)):
                    for j in range(J0):
                        window = bass.AP(tensor=xT[0], offset=(J0 * t0 + j) * CN,
                                         ap=[[CN, F], [J0 * CN, t1 - t0], [1, CN]])
                        sp.dma_start(xb[rows[j], t0:t1, :], window).then_inc(loaded, 16)
                sp.sem_inc(x0_loaded, J0 * 16)

            def load_x0(i, q):
                c = i * 2 + q
                if not known(c, 0):
                    sp.wait_ge(z00_made, c)
                    sp.sem_inc(copies_begun, 1)
                    sp.wait_ge(z0_made, c * (K0 - 1))
                for j in range(J0):
                    rows = slice(j * F, (j + 1) * F)
                    sp.dma_start(xa[rows, :], xT[q].ap()[0:F, :]).then_inc(x0_loaded, 16)
                    window = bass.AP(tensor=xT[q], offset=j * CN, ap=[[CN, F], [J0 * CN, T0], [1, CN]])
                    sp.dma_start(xb[rows, :, :], window).then_inc(x0_loaded, 16)

            def load_xrep(i, q, groups):
                c = i * 2 + q
                for g in groups:
                    back = 2 if g < DOUBLE else 1
                    if not (isinstance(c, int) and c < back):
                        if g in BY_POOL[2]:
                            sp.wait_ge(zb_made, pool_group(2, c - back, g) + 1)
                        elif g == NG1 - 1:
                            sp.wait_ge(zf_made, group(2, c - back, g) + 1)
                        else:
                            sp.wait_ge(zs_made, split_group(2, c - back, g) + 1)
                    slot = xrep_slot(q, g)
                    for a in range(2):
                        n = G - 1 if g == NG1 - 1 and a else G
                        src = bass.AP(tensor=xT[q], offset=(2 * G * g + a) * CN,
                                      ap=[[0, HALF], [2 * CN, n], [1, CN]])
                        sp.dma_start(xrep[a * HALF:(a + 1) * HALF, slot, 0:n, :], src).then_inc(xrep_loaded[slot], 16)
                    if g == NG1 - 1:
                        src = bass.AP(tensor=xT[q], offset=(F - 1) * CN, ap=[[0, HALF], [1, CN]])
                        sp.dma_start(xrep[HALF:P, slot, G - 1, :], src).then_inc(xrep_loaded[slot], 16)

            early, late = range(DOUBLE), range(DOUBLE, NG1)
            transpose_x(0, 0)
            load_first_x0()
            load_xrep(0, 0, range(0, 1))
            transpose_x(0, 1, lambda: load_xrep(0, 0, range(1, 2)))
            load_x0(0, 1)
            load_xrep(0, 0, range(2, NG1))
            sp.wait_ge(pre_left, TOP // P)
            sp.dma_start(pre_dram.ap(), xr1[0]).then_inc(pre_stored, 16)

            def pair(i, first, last):
                for q in range(2):
                    if last and q == 1:
                        break
                    i1, q1 = (i, 1) if q == 0 else (i + 1, 0)
                    if first and q == 0:
                        def rest():
                            sp.wait_ge(pre_stored, 16)
                            sp.sem_inc(copies_begun, 1)
                            load_xrep(0, 1, early)
                        transpose_x(1, 0, rest)
                    else:
                        load_xrep(i1, q1, early)
                        if not last:
                            transpose_x(i + 1, q)
                    if not last:
                        load_x0(i + 1, q)
                    load_xrep(i1, q1, late)

            over_pairs(sp, pair)
            sp.wait_ge(zb_made, pool_group(2, CHUNKS - 2, 1) + 1)
            sp.wait_ge(zs_made, split_group(2, CHUNKS - 2, 0) + 1)
            sp.dma_start(xr[1], pre_dram.ap()).then_inc(top_in, 16)
            sp.dma_start(wt1_sb[0:HALF, 0, :], wt1[HALF:P, :]).then_inc(top_in, 16)
            sp.dma_start(wt1_sb[HALF:P, 0, :], wt1[0:HALF, :]).then_inc(top_in, 16)
            sp.dma_start(wt1_sb[:, 1, :], wt1[P:2 * P, :]).then_inc(top_in, 16)
            sp.dma_start(wt2_sb, wt2.rearrange("(k p) n -> p k n", p=P)).then_inc(top_in, 16)
            sp.wait_ge(y_done, 1)
            sp.dma_start(out.rearrange("b o -> o b"), y_sb).then_inc(y_out, 16)
            sp.wait_ge(y_out, 16)

        @block.gpsimd
        def _(pool):
            def begin_gather(i, q):
                if not known(i, 0):
                    pool.wait_ge(xT_written[q], i * (3 * 16))
                pool.tensor_tensor(rows_sb[:, q, :], ids_sb[:, bass.ds((i * 2 + q) * NG, NG)],
                                   bases_sb[:], ALU.add).then_inc(rows_ready, 1)
                pool.wait_ge(rows_ready, i * 2 + (q + 1))
                pool.sem_inc(gathers_begun, 1)

            def gather(q, gathers):
                for g in gathers:
                    n = min(P, (F - GF * g) * CB)
                    pool.indirect_dma_start(
                        out=emb[0:n, q, g, :], out_offset=None, in_=table,
                        in_offset=bass.IndirectOffsetOnAxis(ap=rows_sb[0:n, q, g:g + 1], axis=0),
                    ).then_inc(gathered[q], 16)

            def product(c, k):
                if k < 2:
                    pool.wait_ge(x0_loaded, (c + 1) * (2 * J0 * 16))
                if not (known(c, 1) and k < 2):
                    pool.wait_ge(lo0_made, (c - 1) * K0 + (k - 1))
                product0(pool, k, z0[:, k % 2])

            def rest_b(layer, c, g):
                pool.wait_ge(hib_made, pool_group(layer, c, g) + 1)
                pool.tensor_tensor(hlb[:, 1], zb[:], hlb[:, 0].bitcast(F32), ALU.subtract).then_inc(lob_made, 1)

            pool.wait_ge(ids_in, 32)
            for c in range(3):
                begin_gather(c // 2, c % 2)
                gather(c % 2, range(NG))
            pool.wait_ge(hl0_free, K0)

            def pair(i, first, last):
                for q in range(2):
                    c = i * 2 + q
                    start = first and q == 0
                    gathers = not known(c, *range(CHUNKS - 3, CHUNKS))
                    if start:
                        product(1, 0)
                        product(1, 1)
                        rest_b(1, 0, 1)
                        rest0(pool, 1, 0)
                        product(1, 2)
                        begin_gather(1, 1)
                        gather(1, range(NG))
                        rest_b(2, 0, 1)
                        product(2, 0)
                        product(2, 1)
                        rest_b(2, 0, 3)
                        rest0(pool, 2, 0)
                        product(2, 2)
                        rest0(pool, 2, 1)
                        rest_b(1, 1, 1)
                        product(2, 3)
                        rest0(pool, 2, 2)
                        rest0(pool, 2, 3)
                        continue
                    if gathers:
                        begin_gather(i + 1 + q, 1 - q)
                        gather(1 - q, range(0, 3))
                    if not known(c, 1):
                        rest_b(1, c, 1)
                    if gathers:
                        gather(1 - q, range(3, NG))
                    if known(c, 1):
                        product(3, 1)
                        rest_b(2, 1, 1)
                        rest0(pool, 3, 0)
                        product(3, 2)
                        rest_b(2, 1, 3)
                        rest0(pool, 3, 1)
                    else:
                        if not last:
                            product(c + 2, 1)
                            rest0(pool, c + 2, 0)
                        rest_b(2, c, 1)
                        if not last:
                            product(c + 2, 2)
                            rest0(pool, c + 2, 1)
                        rest_b(2, c, 3)
                    if not last:
                        product(c + 2, 3)
                        rest0(pool, c + 2, 2)
                        rest0(pool, c + 2, 3)

            pair(0, True, False)
            with pool.Fori(1, PAIRS - 2) as i:
                pair(i, False, False)
            pair(PAIRS - 2, False, False)
            pair(PAIRS - 1, False, True)

        @block.vector
        def _(dve):
            h_of = {1: h1, 2: h2}

            def products(dst, layer, c, q, g, half, made):
                in0 = xrep[:, xrep_slot(q, g), half * H:(half + 1) * H, :]
                dve.tensor_tensor(dst, in0, h_of[layer][:].unsqueeze(1).to_broadcast([P, H, CN]),
                                  ALU.mult).then_inc(made, 1)

            def float_products(layer, c, q, g):
                dve.wait_ge(zf_free, group(layer, c, g) + 1)
                products(zf[:, next(zf_slots)], layer, c, q, g, 1 - split_half(g), zf_made)

            def split_products(layer, c, q, g):
                if g in BY_POOL[layer]:
                    at = pool_group(layer, c, g)
                    if not known(at, 0):
                        dve.wait_ge(lob_made, at)
                    products(zb[:], layer, c, q, g, split_half(g), zb_made)
                    return
                at = split_group(layer, c, g)
                if not known(at, 0, 1):
                    dve.wait_ge(lo_made, at - 1)
                products(zs[:, made[0] % 2], layer, c, q, g, split_half(g), zs_made)
                made[0] += 1

            def group_rest(layer, c, g, back):
                n = made[0] - 1 - back
                dve.wait_ge(hi_made, split_group(layer, c, g) + 1)
                dve.tensor_tensor(hl[:, n % HL_RING, 1], zs[:, n % 2], hl[:, n % HL_RING, 0].bitcast(F32),
                                  ALU.subtract).then_inc(lo_made, 1)

            def stage(layer, c, q, loaded=None):
                waiting = None
                for g in range(NG1):
                    if loaded is not None:
                        dve.wait_ge(*loaded(g))
                    if layer == 2 and g == NG1 - 1:
                        split_products(layer, c, q, g)
                        float_products(layer, c, q, g)
                    else:
                        float_products(layer, c, q, g)
                        split_products(layer, c, q, g)
                    if waiting is not None:
                        group_rest(layer, c, waiting, 0 if g in BY_POOL[layer] else 1)
                        waiting = None
                    if g not in BY_POOL[layer]:
                        waiting = g
                group_rest(layer, c, waiting, 0)

            def sum_over_d(sums, direct, c, done):
                dve.tensor_reduce(sums[:, bass.ds(c * CB, CB)],
                                  direct.rearrange("p (b d) -> p b d", d=D), AX_X,
                                  ALU.add).then_inc(done, 1)

            def layer2_sums(c):
                dve.wait_ge(direct2_ready, c + 1)
                sum_over_d(sums2, direct2[:], c, sums2_done)

            def layer01_sums(c, q):
                dve.wait_ge(direct01_ready, (c + 1) * 2)
                sum_over_d(sums01, direct01[:, q], c, sums01_done)

            dve.wait_ge(w0_in, 32)
            dve.tensor_tensor(w0f, w0f, w0_in1, ALU.add).then_inc(w_step, 1)
            dve.wait_ge(w_hi, 3)
            for w, src in zip(w_parts, w_whole):
                dve.tensor_tensor(w[1], src, w[0].bitcast(F32), ALU.subtract).then_inc(w_step, 1)
            dve.wait_ge(w_step, 4)
            for w in (w1_sb, w2_sb):
                dve.tensor_copy(w[HALF:P, 0, NG1 - 1, H - 1, :],
                                w[HALF:P, 1, NG1 - 1, H - 1, :].bitcast(F32)).then_inc(w_step, 1)
            for k in range(K0):
                dve.wait_ge(*((x0_first[0], 2 * J0 * 16), (x0_first[1], J0 * 16), (x0_loaded, 2 * J0 * 16))[min(k, 2)])
                product0(dve, k, z_first[k])
            dve.wait_ge(pre_left, TOP // P)
            zf_slots = cycle(range(C_RING))
            made = [0]

            def pair(i, first, last):
                for q in range(2):
                    c = i * 2 + q
                    dve.wait_ge(h1_ready, (c + 1) * 2)
                    stage(1, c, q, lambda g: (xrep_loaded[xrep_slot(q, g)],
                                              (i + 1 if g < DOUBLE else c + 1) * (xrep_loads(g) * 16)))
                    if not (first and q == 0):
                        layer2_sums(c - 1)
                        layer01_sums(c - 1, 1 - q)
                        if not last:
                            dve.wait_ge(lo0_made, c * K0 + 3)
                            dve.wait_ge(x0_loaded, (c + 3) * (2 * J0 * 16))
                            product0(dve, 0, z0[:, 0])
                    else:
                        dve.wait_ge(lo0_made, 1)
                        rest0(dve, 1, 1)
                        dve.wait_ge(hi0_made, 3)
                        dve.wait_ge(lo0_made, 2)
                        product0(dve, 3, z0[:, 1])
                        rest0(dve, 1, 2)
                        rest0(dve, 1, 3)
                    dve.wait_ge(h2_ready, (c + 1) * 2)
                    stage(2, c, q)

            over_pairs(dve, pair)
            layer01_sums(CHUNKS - 1, 1)
            layer2_sums(CHUNKS - 1)
            dve.wait_ge(top_in, 5 * 16)
            for m in range(TOP // P):
                dve.wait_ge(top_done, m + 1)
                dve.tensor_tensor(pre_sb[:, m, :], top_banks[m][:], pre_sb[:, m, :], ALU.add).then_inc(top_sum, 1)

        @block.tensor
        def _(pe):
            pe.sem_inc(zf_free, C_RING)
            pe.sem_inc(hl_free, HL_RING)
            banks = cycle(acc)
            zf_slots = cycle(range(C_RING))
            used = [0]

            def first_layer0():
                bank = next(banks)
                for k in range(K0):
                    pe.wait_ge(*((z0_made, k) if k else (z00_made, 1)))
                    for u in range(tiles0(k)):
                        t = H * k + u
                        rows = R0_LAST if t == T0 - 1 else R0
                        mm = pe.matmul(bank[:], w0f_tiles[0:rows, t, :], z_first[k][0:rows, u, :],
                                       start=(t == 0), stop=(t == T0 - 1))
                    mm.then_inc(hl0_free, 1)

            def layer0(c, bank_read):
                bank = next(banks)
                pe.wait_ge(*bank_read)
                for k in range(K0):
                    n = tiles0(k)
                    pe.wait_ge(hi0_made, (c - 1) * K0 + (k + 1))
                    for part_w, part_z in ((1, 0), (0, 0), (0, 1)):
                        if part_z:
                            pe.wait_ge(lo0_made, (c - 1) * K0 + (k + 1))
                        for u in range(n):
                            t = H * k + u
                            rows = R0_LAST if t == T0 - 1 else R0
                            mm = pe.matmul(bank[:], w0_sb[0:rows, part_w, t, :], hl0[0:rows, k, part_z, u, :],
                                           start=(t == 0 and part_w == 1),
                                           stop=(t == T0 - 1 and part_z == 1))
                    mm.then_inc(hl0_free, 1)

            def layer12(layer, c, bank_read):
                w, wf = ((w1_sb, w1f_sb), (w2_sb, w2f_sb))[layer - 1]
                bank = next(banks)
                pe.wait_ge(*bank_read)
                def split_pass(g, parts, part_w, part_z, stop=False):
                    for u in range(H):
                        rows = P
                        if g == NG1 - 1 and u == H - 1:
                            if part_w:
                                continue
                            rows = HALF if part_z else P
                        mm = pe.matmul(bank[:], w[0:rows, part_w, g, u, :], parts[0:rows, part_z, u, :],
                                       start=False, stop=(stop and u == H - 1))
                    return mm

                def rest_pass(g, back, stop=False):
                    pe.wait_ge(lo_made, split_group(layer, c, g) + 1)
                    split_pass(g, hl[:, (used[0] - 1 - back) % HL_RING], 0, 1, stop).then_inc(hl_free, 1)

                def pool_passes(g, stop=False):
                    pe.wait_ge(lob_made, pool_group(layer, c, g) + 1)
                    split_pass(g, hlb, 1, 0)
                    split_pass(g, hlb, 0, 0)
                    split_pass(g, hlb, 0, 1, stop).then_inc(hlb_free, 1)

                waiting = None
                for g in range(NG1):
                    if g == (NG1 - 1 if layer == 1 else 3):
                        pool_passes(1)
                    pe.wait_ge(zf_made, group(layer, c, g) + 1)
                    slot = next(zf_slots)
                    for u in range(H):
                        mm = pe.matmul(bank[:], wf[:, g, u, :], zf[:, slot, u, :],
                                       start=(g == 0 and u == 0), stop=False)
                    mm.then_inc(zf_free, 1)
                    if g not in BY_POOL[layer]:
                        pe.wait_ge(hi_made, split_group(layer, c, g) + 1)
                        parts = hl[:, used[0] % HL_RING]
                        used[0] += 1
                        split_pass(g, parts, 1, 0)
                        split_pass(g, parts, 0, 0)
                    if waiting is not None:
                        rest_pass(waiting, 0 if g in BY_POOL[layer] else 1)
                        waiting = None
                    if g not in BY_POOL[layer]:
                        waiting = g
                rest_pass(waiting, 0, stop=(layer == 1))
                if layer == 2:
                    pool_passes(3, stop=True)

            def top1_pass(m, k, c0, c1):
                return pe.matmul(top_banks[m][:, c0:c1], wt1_sb[:, k, m * P:(m + 1) * P],
                                 (sums01, sums2)[k][:, c0:c1], start=(k == 0), stop=(k == 1))

            pe.wait_ge(dense_in, 32)
            pe.wait_ge(w_hi, 1)
            for m in range(TOP // P):
                pe.matmul(zs[:, m // 2, m % 2, :], wt1d_sb[:, m * P:(m + 1) * P], dense_sb, start=True,
                          stop=True).then_inc(dense_done, 1)
            pe.wait_ge(w_step, 6)
            first_layer0()

            def pair(i, first, last):
                for q in range(2):
                    c = i * 2 + q
                    end = last and q == 1
                    layer12(1, c, (w12_in, 64) if first and q == 0 else (direct01_ready, c * 2 + 1))
                    if not end:
                        layer0(c + 1, (direct01_ready, 1) if first and q == 0 else (direct2_ready, c))
                    else:
                        pe.wait_ge(top_in, 5 * 16)
                        pe.wait_ge(sums01_done, CHUNKS - 1)
                        pe.wait_ge(sums2_done, CHUNKS - 1)
                        next(banks)
                        for m in range(2):
                            for k in range(2):
                                top1_pass(m, k, 0, B - CB)
                    layer12(2, c, (direct01_ready, c * 2 + 2))

            over_pairs(pe, pair)

            pe.wait_ge(sums01_done, CHUNKS)
            for m in range(TOP // P):
                top1_pass(m, 0, B - CB if m < 2 else 0, B)
            pe.wait_ge(sums2_done, CHUNKS)
            for m in range(TOP // P):
                top1_pass(m, 1, B - CB if m < 2 else 0, B).then_inc(top_done, 1)
            pe.wait_ge(top_small_in, 3 * 16)
            for k in range(TOP // P):
                pe.wait_ge(top_relu, k + 1)
                for m in range(TOP2 // P):
                    mm = pe.matmul(zs[:, 1, m, :], wt2_sb[:, k, m * P:(m + 1) * P], top1[:, k, :],
                                   start=(k == 0), stop=(k == TOP // P - 1))
                    if k == TOP // P - 1:
                        mm.then_inc(top_done, 1)
            for k in range(TOP2 // P):
                pe.wait_ge(top_relu, TOP // P + k + 1)
                mm = pe.matmul(acc[0][0:1, :], wt3_sb[:, k:k + 1], top2[:, k, :],
                               start=(k == 0), stop=(k == TOP2 // P - 1))
            mm.then_inc(top_done, 1)

        @block.scalar
        def _(act):
            lo, hi = slice(0, HALF), slice(HALF, P)
            banks = cycle(acc)
            made = [0]

            def relu(dst, src, rows, layer):
                return act.activation(dst, src, ACT.Relu, bias=bias_sb[rows, layer:layer + 1])

            def split0(c, k):
                n = tiles0(k)
                act.wait_ge(hl0_free, (c - 1) * K0 + (k + 1))
                if k == 0:
                    act.wait_ge(z00_made, c + 1)
                else:
                    act.wait_ge(z0_made, c * (K0 - 1) + k)
                act.copy(hl0[:, k, 0, 0:n, :], z0[:, k % 2, 0:n, :]).then_inc(hi0_made, 1)

            def split12(layer, c, g):
                if g in BY_POOL[layer]:
                    at = pool_group(layer, c, g)
                    if not known(at, 0):
                        act.wait_ge(hlb_free, at)
                    act.wait_ge(zb_made, at + 1)
                    act.copy(hlb[:, 0], zb[:]).then_inc(hib_made, 1)
                    return
                at = split_group(layer, c, g)
                act.wait_ge(hl_free, at + 1)
                act.wait_ge(zs_made, at + 1)
                act.copy(hl[:, made[0] % HL_RING, 0], zs[:, made[0] % 2]).then_inc(hi_made, 1)
                made[0] += 1

            def layer0(c, q):
                bank = next(banks)
                act.wait_ge(hl0_free, (c + 1) * K0)
                if not known(c, 0):
                    act.wait_ge(zs_made, split_group(1, c - 1, NG1))
                relu(h1[lo, :], bank[lo, :], lo, 0).then_inc(h1_ready, 1)
                relu(h1[hi, :], bank[lo, :], lo, 0).then_inc(h1_ready, 1)
                if not known(c, 0, 1):
                    act.wait_ge(sums01_done, c - 1)
                relu(direct01[hi, q, :], bank[hi, :], hi, 0).then_inc(direct01_ready, 1)

            def layer1(c, q):
                bank = next(banks)
                act.wait_ge(hl_free, split_group(1, c, NG1) + HL_RING)
                if not known(c, 0):
                    act.wait_ge(zf_made, group(2, c - 1, NG1))
                relu(h2[lo, :], bank[lo, :], lo, 1).then_inc(h2_ready, 1)
                relu(h2[hi, :], bank[lo, :], lo, 1).then_inc(h2_ready, 1)
                relu(direct01[lo, q, :], bank[hi, :], hi, 1).then_inc(direct01_ready, 1)

            def layer2(c, bank):
                act.wait_ge(hlb_free, pool_group(2, c, NG1))
                if not known(c, 0):
                    act.wait_ge(sums2_done, c)
                relu(direct2[:], bank[:], slice(0, P), 2).then_inc(direct2_ready, 1)

            act.wait_ge(small_in, 16)
            act.wait_ge(w12_in, 64)
            act.wait_ge(w_step, 1)
            for w, src in zip(w_parts, w_whole):
                act.copy(w[0], src).then_inc(w_hi, 1)
            for m in range(TOP // P):
                act.wait_ge(dense_done, m + 1)
                act.copy(pre_first[:, m, :], zs[:, m // 2, m % 2, :]).then_inc(pre_left, 1)
            layer0(0, 0)
            layer2_bank = [None]

            def pair(i, first, last):
                for q in range(2):
                    c = i * 2 + q
                    start = first and q == 0
                    for g in range(NG1):
                        split12(1, c, g)
                        if start and g >= 2:
                            split0(1, g - 2)
                        if known(c, 1):
                            if g in (0, 2):
                                split0(2, 2 + g // 2)
                        elif g == 0 and not start and not (last and q == 1):
                            split0(c + 1, 3)
                        if g == 2 and not start:
                            layer2(c - 1, layer2_bank[0])
                    if start:
                        split0(1, 3)
                    layer1(c, q)
                    if not last and not start:
                        split0(c + 2, 0)
                    if last and q == 1:
                        next(banks)
                    for g in range(NG1):
                        split12(2, c, g)
                        if g == 2 and not (last and q == 1):
                            layer0(c + 1, 1 - q)
                        if g in (1, 4) and not last and not start:
                            split0(c + 2, 1 + g // 4)
                        if g >= 3 and start:
                            split0(2, g - 3)
                    layer2_bank[0] = next(banks)

            over_pairs(act, pair)
            layer2(CHUNKS - 1, layer2_bank[0])

            act.wait_ge(top_small_in, 3 * 16)
            for m in range(TOP // P):
                act.wait_ge(top_sum, m + 1)
                act.activation(top1[:, m, :], pre_sb[:, m, :], ACT.Relu,
                               bias=bt1_sb[:, m:m + 1]).then_inc(top_relu, 1)
            for m in range(TOP2 // P):
                act.wait_ge(top_done, TOP // P + m + 1)
                act.activation(top2[:, m, :], zs[:, 1, m, :], ACT.Relu,
                               bias=bt2_sb[:, m:m + 1]).then_inc(top_relu, 1)
            act.wait_ge(top_done, TOP // P + TOP2 // P + 1)
            act.copy(y_sb, acc[0][0:1, :]).then_inc(y_done, 1)


def kernel(**inputs):
    import numpy as np
    import concourse.bacc as bacc
    from concourse.bass_utils import run_bass_kernel_spmd

    a = {n: np.asarray(v) for n, v in inputs.items()}
    tables = [a[f"tbl_{f}"] for f in range(F)]
    first_row = np.cumsum([0] + [t.shape[0] for t in tables[:-1]])

    ids = np.zeros((B, NG * GF), np.int32)
    ids[:, :F] = a["ids"]
    ids = ids.reshape(CHUNKS, CB, NG, GF).transpose(3, 1, 0, 2).reshape(P, CHUNKS * NG)
    bases = np.zeros(NG * GF, np.int32)
    bases[:F] = first_row
    bases = np.repeat(bases.reshape(NG, GF).T, CB, axis=0)

    w0 = a["L0_rec_W0"].reshape(F, F, L)
    w0a = np.zeros((J0, F, T0, L), w0.dtype)
    w0b = np.zeros((J0, F, T0, L), w0.dtype)
    f = np.arange(F)
    for k in range(OFFS):
        t, j = divmod(k, J0)
        w0a[j, :, t] = w0[f, (f + k) % F]
        if k:
            w0b[j, :, t] = w0[(f + k) % F, f]

    w12 = []
    for name in ("L0_rec_W1", "L0_rec_W2"):
        w = np.concatenate([a[name], a[name][-HALF:]]).reshape(NG1, 2, H, P, L)
        w[-1] = w[-1, ::-1].copy()
        w = w.transpose(1, 3, 0, 2, 4).reshape(2, P, NG1 * H * L)
        w12.append((w[0], w[1]))

    arrays = {
        "table": np.concatenate(tables, axis=0),
        "ids": ids,
        "bases": bases,
        "w0a": w0a.reshape(R0, T0, L),
        "w0b": w0b.reshape(R0, T0, L),
        "w1s": w12[0][0],
        "w1f": w12[0][1],
        "w2s": w12[1][0],
        "w2f": w12[1][1],
        "biases": np.stack([a["L0_rec_b0"], a["L0_rec_b1"], a["L0_rec_b2"]], axis=1),
        "denseT": a["dense_ctx"].T,
        "wt1": a["W_top1"],
        "bt1": a["b_top1"].reshape(TOP // P, P).T,
        "wt2": a["W_top2"],
        "bt2": a["b_top2"].reshape(TOP2 // P, P).T,
        "wt3": a["W_top3"].reshape(TOP2 // P, P).T,
    }
    arrays = {n: np.ascontiguousarray(v) for n, v in arrays.items()}
    nc = bacc.Bacc("TRN2", target_bir_lowering=False, num_devices=1)
    args = {n: nc.dram_tensor(n, v.shape, mybir.dt.from_np(v.dtype), kind="ExternalInput").ap()
            for n, v in arrays.items()}
    y = nc.dram_tensor("y", (B, 1), F32, kind="ExternalOutput").ap()
    build(nc, out=y, **args)
    r = run_bass_kernel_spmd(nc, [arrays], core_ids=[0])
    return r.results[0]["y"]
```
